# Optimizing a Trainium2 kernel written in Bass

```python
import numpy as np
import jax
import jax.numpy as jnp

def _softmax(x, axis=-1):
    return jax.nn.softmax(x, axis=axis)

def _gelu(x):
    return jax.nn.gelu(x, approximate=True)

def _silu(x):
    return jax.nn.silu(x)

def _sigmoid(x):
    return jax.nn.sigmoid(x)

def _layernorm(x, axis=-1, eps=1e-05):
    m = jnp.mean(x, axis=axis, keepdims=True)
    v = jnp.var(x, axis=axis, keepdims=True)
    return (x - m) / jnp.sqrt(v + eps)

def _scatter_add(tgt, idx, src, axis=0):
    return tgt.at[idx].add(src)

def _segment_sum(src, seg, n):
    return jax.ops.segment_sum(src, seg, n)
kernel_name = 'mk_lm_tower_d1_tok_ids256_r4_a6a9c9'

def setup_inputs(seed: int=0):
    np.random.seed(seed)
    _w = jnp.asarray

    def _rec_inputs():
        import jax
        import jax.numpy as jnp
        _rk = jax.random.key(seed)
        x = jax.random.randint(jax.random.fold_in(_rk, 1), (4, 512), 0, 12564, jnp.int32)
        return x
    x = _rec_inputs()

    def _L0_tok_setup():
        import jax, jax.numpy as jnp
        import numpy as np
        VOCAB = 50257
        C = 5
        D = 64
        B = 8
        S = 1024
        key = jax.random.key(seed)
        k1, k2 = jax.random.split(key)
        x = jax.random.randint(k1, (B, S), 0, VOCAB, dtype=jnp.int32)
        emb_table = jax.random.normal(k2, (VOCAB, C, D), dtype=jnp.float32) * 0.02
        return {'x': x, 'emb_table': emb_table}
    _L0_tok_all = _L0_tok_setup()
    _L0_tok_in = {k: v for k, v in _L0_tok_all.items() if k in ('emb_table',)}
    del _L0_tok_all

    def _L0_attn_setup():
        import jax, jax.numpy as jnp
        import numpy as np
        import math
        B, T, D_MODEL = (1, 512, 64)
        N_Q, N_KV = (16, 1)
        D_HEAD = D_MODEL // N_KV
        QPG = N_Q // N_KV
        ROPE_BASE = 10000.0
        WINDOW = 128
        EPS = 1.1920929e-07
        NEG = -1e+30

        def _rope(x, base=ROPE_BASE):
            t, d = (x.shape[-2], x.shape[-1])
            freqs = base ** (-2.0 * jnp.arange(d // 2, dtype=jnp.float32) / d)
            theta = jnp.arange(t, dtype=jnp.float32)[:, None] * freqs[None, :]
            cos, sin = (jnp.cos(theta), jnp.sin(theta))
            x1, x2 = (x[..., 0::2], x[..., 1::2])
            r1 = x1 * cos - x2 * sin
            r2 = x1 * sin + x2 * cos
            return jnp.stack([r1, r2], axis=-1).reshape(x.shape)

        def _rmsnorm(x, w):
            return x * jax.lax.rsqrt(jnp.mean(x * x, axis=-1, keepdims=True) + EPS) * w
        key = jax.random.key(seed)
        k0, k1, k2, k3 = jax.random.split(key, 4)
        x = jax.random.normal(k0, (B, T, D_MODEL), dtype=jnp.float32)
        wq = jax.random.normal(k1, (QPG * N_KV * D_HEAD, D_MODEL), dtype=jnp.float32) * 0.02
        wkv = jax.random.normal(k2, (2 * D_HEAD * N_KV, D_MODEL), dtype=jnp.float32) * 0.02
        wo = jax.random.normal(k3, (D_MODEL, D_HEAD * N_Q * N_KV), dtype=jnp.float32) * 0.02
        q_norm_w = jnp.ones((D_HEAD,), dtype=jnp.float32)
        k_norm_w = jnp.ones((D_HEAD,), dtype=jnp.float32)
        return {'x': x, 'wq': wq, 'wkv': wkv, 'wo': wo, 'q_norm_w': q_norm_w, 'k_norm_w': k_norm_w}
    _L0_attn_all = _L0_attn_setup()
    _L0_attn_in = {k: v for k, v in _L0_attn_all.items() if k in ('wq', 'wkv', 'wo', 'q_norm_w', 'k_norm_w')}
    del _L0_attn_all

    def _L0_ffn_setup():
        import jax, jax.numpy as jnp
        import numpy as np
        B, A = (1024, 8)
        IN, OUT = (64, 64)
        SH1, SH2 = (64, 128)
        EH1, EH2 = (128, 64)
        E, TOPK = (4, 2)

        def _shared_mlp(x, W1, b1, W2, b2, W3, b3):
            h = jax.nn.relu(x @ W1 + b1)
            h = jax.nn.relu(h @ W2 + b2)
            return h @ W3 + b3

        def _experts_mlp(x, eW1, eb1, eW2, eb2, eW3, eb3):
            h = jax.nn.relu(jnp.einsum('baf,efh->ebah', x, eW1) + eb1[:, None, None, :])
            h = jax.nn.relu(jnp.einsum('ebah,ehg->ebag', h, eW2) + eb2[:, None, None, :])
            o = jnp.einsum('ebag,ego->ebao', h, eW3) + eb3[:, None, None, :]
            return jnp.moveaxis(o, 0, -1)
        key = jax.random.key(seed)
        ks = jax.random.split(key, 16)
        s = 0.05
        return {'x': jax.random.normal(ks[0], (B, A, IN), jnp.float32), 'sW1': jax.random.normal(ks[1], (IN, SH1), jnp.float32) * s, 'sb1': jnp.zeros((SH1,), jnp.float32), 'sW2': jax.random.normal(ks[2], (SH1, SH2), jnp.float32) * s, 'sb2': jnp.zeros((SH2,), jnp.float32), 'sW3': jax.random.normal(ks[3], (SH2, OUT), jnp.float32) * s, 'sb3': jnp.zeros((OUT,), jnp.float32), 'eW1': jax.random.normal(ks[4], (E, IN, EH1), jnp.float32) * s, 'eb1': jnp.zeros((E, EH1), jnp.float32), 'eW2': jax.random.normal(ks[5], (E, EH1, EH2), jnp.float32) * s, 'eb2': jnp.zeros((E, EH2), jnp.float32), 'eW3': jax.random.normal(ks[6], (E, EH2, OUT), jnp.float32) * s, 'eb3': jnp.zeros((E, OUT), jnp.float32), 'gW': jax.random.normal(ks[7], (IN, E), jnp.float32) * s, 'gb': jnp.zeros((E,), jnp.float32)}
    _L0_ffn_all = _L0_ffn_setup()
    _L0_ffn_in = {k: v for k, v in _L0_ffn_all.items() if k in ('sW1', 'sb1', 'sW2', 'sb2', 'sW3', 'sb3', 'eW1', 'eb1', 'eW2', 'eb2', 'eW3', 'eb3', 'gW', 'gb')}
    del _L0_ffn_all
    return {'x': x, 'L0_tok_emb_table': _L0_tok_in['emb_table'], 'L0_attn_wq': _L0_attn_in['wq'], 'L0_attn_wkv': _L0_attn_in['wkv'], 'L0_attn_wo': _L0_attn_in['wo'], 'L0_attn_q_norm_w': _L0_attn_in['q_norm_w'], 'L0_attn_k_norm_w': _L0_attn_in['k_norm_w'], 'L0_ffn_sW1': _L0_ffn_in['sW1'], 'L0_ffn_sb1': _L0_ffn_in['sb1'], 'L0_ffn_sW2': _L0_ffn_in['sW2'], 'L0_ffn_sb2': _L0_ffn_in['sb2'], 'L0_ffn_sW3': _L0_ffn_in['sW3'], 'L0_ffn_sb3': _L0_ffn_in['sb3'], 'L0_ffn_eW1': _L0_ffn_in['eW1'], 'L0_ffn_eb1': _L0_ffn_in['eb1'], 'L0_ffn_eW2': _L0_ffn_in['eW2'], 'L0_ffn_eb2': _L0_ffn_in['eb2'], 'L0_ffn_eW3': _L0_ffn_in['eW3'], 'L0_ffn_eb3': _L0_ffn_in['eb3'], 'L0_ffn_gW': _L0_ffn_in['gW'], 'L0_ffn_gb': _L0_ffn_in['gb']}

def reference(x, L0_tok_emb_table, L0_attn_wq, L0_attn_wkv, L0_attn_wo, L0_attn_q_norm_w, L0_attn_k_norm_w, L0_ffn_sW1, L0_ffn_sb1, L0_ffn_sW2, L0_ffn_sb2, L0_ffn_sW3, L0_ffn_sb3, L0_ffn_eW1, L0_ffn_eb1, L0_ffn_eW2, L0_ffn_eb2, L0_ffn_eW3, L0_ffn_eb3, L0_ffn_gW, L0_ffn_gb):
    import jax
    import jax.numpy as jnp

    def _L0_tok_ref(x, emb_table):
        import jax, jax.numpy as jnp
        import numpy as np
        VOCAB = 50257
        C = 5
        D = 64
        B = 8
        S = 1024
        Bn, Sn = x.shape
        _, Cn, Dn = emb_table.shape
        x_pad = jnp.concatenate([x, jnp.zeros((Bn, Cn), dtype=x.dtype)], axis=1)
        out = emb_table[x_pad[:, 0:Sn], 0]
        for i in range(1, Cn):
            out = out + emb_table[x_pad[:, i:Sn + i], i]
        return out

    def _L0_attn_ref(x, wq, wkv, wo, q_norm_w, k_norm_w):
        import jax, jax.numpy as jnp
        import numpy as np
        import math
        B, T, D_MODEL = (1, 512, 64)
        N_Q, N_KV = (16, 1)
        D_HEAD = D_MODEL // N_KV
        QPG = N_Q // N_KV
        ROPE_BASE = 10000.0
        WINDOW = 128
        EPS = 1.1920929e-07
        NEG = -1e+30

        def _rope(x, base=ROPE_BASE):
            t, d = (x.shape[-2], x.shape[-1])
            freqs = base ** (-2.0 * jnp.arange(d // 2, dtype=jnp.float32) / d)
            theta = jnp.arange(t, dtype=jnp.float32)[:, None] * freqs[None, :]
            cos, sin = (jnp.cos(theta), jnp.sin(theta))
            x1, x2 = (x[..., 0::2], x[..., 1::2])
            r1 = x1 * cos - x2 * sin
            r2 = x1 * sin + x2 * cos
            return jnp.stack([r1, r2], axis=-1).reshape(x.shape)

        def _rmsnorm(x, w):
            return x * jax.lax.rsqrt(jnp.mean(x * x, axis=-1, keepdims=True) + EPS) * w
        Bx, Tx, C = x.shape
        q = x @ wq.T
        kv = x @ wkv.T
        k, v = (kv[..., :N_KV * D_HEAD], kv[..., N_KV * D_HEAD:])
        q = q.reshape(Bx, Tx, QPG, N_KV, D_HEAD).transpose(0, 2, 3, 1, 4)
        k = k.reshape(Bx, Tx, 1, N_KV, D_HEAD).transpose(0, 2, 3, 1, 4)
        v = v.reshape(Bx, Tx, 1, N_KV, D_HEAD).transpose(0, 2, 3, 1, 4)
        q = _rmsnorm(_rope(q), q_norm_w)
        k = _rmsnorm(_rope(k), k_norm_w)
        rows = jnp.arange(Tx)[:, None]
        cols = jnp.arange(Tx)[None, :]
        mask = (cols <= rows) & (rows - cols <= WINDOW)
        scale = 1.0 / math.sqrt(D_HEAD)
        scores = jnp.einsum('bqgtd,bqgsd->bqgts', q, k) * scale
        scores = jnp.where(mask[None, None, None], scores, NEG)
        attn = jax.nn.softmax(scores, axis=-1)
        out = jnp.einsum('bqgts,bqgsd->bqgtd', attn, v)
        out = out.transpose(0, 3, 1, 2, 4).reshape(Bx, Tx, QPG * N_KV * D_HEAD)
        return out @ wo.T

    def _L0_ffn_ref(x, sW1, sb1, sW2, sb2, sW3, sb3, eW1, eb1, eW2, eb2, eW3, eb3, gW, gb):
        import jax, jax.numpy as jnp
        import numpy as np
        B, A = (1024, 8)
        IN, OUT = (64, 64)
        SH1, SH2 = (64, 128)
        EH1, EH2 = (128, 64)
        E, TOPK = (4, 2)

        def _shared_mlp(x, W1, b1, W2, b2, W3, b3):
            h = jax.nn.relu(x @ W1 + b1)
            h = jax.nn.relu(h @ W2 + b2)
            return h @ W3 + b3

        def _experts_mlp(x, eW1, eb1, eW2, eb2, eW3, eb3):
            h = jax.nn.relu(jnp.einsum('baf,efh->ebah', x, eW1) + eb1[:, None, None, :])
            h = jax.nn.relu(jnp.einsum('ebah,ehg->ebag', h, eW2) + eb2[:, None, None, :])
            o = jnp.einsum('ebag,ego->ebao', h, eW3) + eb3[:, None, None, :]
            return jnp.moveaxis(o, 0, -1)
        all_out = _experts_mlp(x, eW1, eb1, eW2, eb2, eW3, eb3)
        shared = _shared_mlp(x, sW1, sb1, sW2, sb2, sW3, sb3)
        gates = jax.nn.softmax(x @ gW + gb, axis=-1)
        topv, topi = jax.lax.top_k(gates, TOPK)
        topw = jax.nn.softmax(topv, axis=-1)
        sel = jnp.take_along_axis(all_out, topi[:, :, None, :], axis=-1)
        gated = jnp.sum(sel * topw[:, :, None, :], axis=-1)
        return shared + gated
    h = _L0_tok_ref(x, L0_tok_emb_table)
    h = h + _L0_attn_ref(_layernorm(h, axis=-1), L0_attn_wq, L0_attn_wkv, L0_attn_wo, L0_attn_q_norm_w, L0_attn_k_norm_w)
    h = h + _L0_ffn_ref(_layernorm(h, axis=-1), L0_ffn_sW1, L0_ffn_sb1, L0_ffn_sW2, L0_ffn_sb2, L0_ffn_sW3, L0_ffn_sb3, L0_ffn_eW1, L0_ffn_eb1, L0_ffn_eW2, L0_ffn_eb2, L0_ffn_eW3, L0_ffn_eb3, L0_ffn_gW, L0_ffn_gb)
    return h

_drawn_inputs = setup_inputs


def setup_inputs(seed=0):
    import zlib

    import numpy as np

    out = dict(_drawn_inputs(seed))
    spreads = {'L0_attn_q_norm_w': (1.0, 0.2),
     'L0_attn_k_norm_w': (1.0, 0.2),
     'L0_ffn_sb1': (0.0, 0.1),
     'L0_ffn_sb2': (0.0, 0.1),
     'L0_ffn_sb3': (0.0, 0.1),
     'L0_ffn_eb1': (0.0, 0.1),
     'L0_ffn_eb2': (0.0, 0.1),
     'L0_ffn_eb3': (0.0, 0.1),
     'L0_ffn_gb': (0.0, 0.1)}
    factors = {}
    for name, (base, spread) in spreads.items():
        noise = np.random.default_rng([zlib.crc32(name.encode()), seed]).standard_normal(out[name].shape)
        drawn = base * np.exp(spread * noise) if base else spread * noise
        out[name] = jnp.asarray(drawn.astype(out[name].dtype))
    for name, factor in factors.items():
        out[name] = (out[name] * factor).astype(out[name].dtype)
    return out
```

```python
import concourse.bass as bass
import concourse.mybir as mybir
import numpy as np
from contextlib import ExitStack

FP32 = mybir.dt.float32
BF16 = mybir.dt.bfloat16
I32 = mybir.dt.int32
ALU = mybir.AluOpType
ACT = mybir.ActivationFunctionType
AX = mybir.AxisListType

B, S, D = 4, 512, 64
C = 5
H = 16
PAIRS = H // 2
P = 128
TILES = S // P
SLOTS = S // P
WIN = 2 * P
E, EH1, EH2, SH1, SH2 = 4, 128, 64, 64, 128
LN_EPS, RMS_EPS = 1e-5, 1.1920929e-07
NEG = -1e30

def _columns(parts):
    at, where = 0, {}
    for name, width in parts:
        where[name] = (at, width)
        at += width
    return where, at

EARLY, EARLY_W = _columns([("ident", P), ("trig", S), ("k_cos", TILES * D), ("k_sin", TILES * D),
                           ("swap_sign", D), ("qn", D), ("kn", D), ("ident2", D)])
LATE, LATE_W = _columns([("wo", PAIRS * D), ("eW2", E * EH2), ("sW3", D), ("eW3", 2 * P), ("eb1", E),
                         ("eb2", 2), ("sb2", 1), ("sb1", 1), ("eb3", E * D), ("sb3", D), ("before", E * E)])
W64, W64_W = _columns([("wq", H * D), ("wkv", 2 * D), ("sW1", SH1), ("eW1", E * EH1), ("sW2", SH2), ("gW", E)])


def build(nc, tok, table, early_d, mask_d, late_d, w64_d, gb_d, out):
    with ExitStack() as ctx:
        def sb(name, shape, dt=FP32):
            return ctx.enter_context(nc.sbuf_tensor(name, shape, dt))

        def sem(name):
            return ctx.enter_context(nc.semaphore(name))

        idx = sb("idx", [P, B * SLOTS], I32)
        emb = sb("emb", [P, B, 2 * SLOTS, C * D])
        early = sb("early", [P, EARLY_W])
        late = sb("late", [P, LATE_W])
        w64 = sb("w64", [D + 1, W64_W])
        mask = sb("mask", [P, 2 * WIN], BF16)
        identb = sb("identb", [P, P], BF16)
        ones = sb("ones", [P, D])
        gs = sb("gs", [P, D])
        shift = sb("shift", [P, 2])
        h = sb("h", [P, B, SLOTS, D])
        xc = sb("xc", [P, SLOTS, D])
        sq = sb("sq", [P, SLOTS, D])
        xn = sb("xn", [P, SLOTS, D])
        stat = sb("stat", [P, 8, SLOTS])
        xT = sb("xT", [D + 1, S])
        kq = sb("kq", [P, 4, TILES, D])
        kstat = sb("kstat", [P, 3, TILES])
        ktok = sb("ktok", [P, TILES, 2, D])
        kst = sb("kst", [P, S])
        v_next = sb("v_next", [P, TILES, D])
        v = sb("v", [P, TILES, D])
        qsq = sb("qsq", [P, H, D])
        qstat = sb("qstat", [P, 3, H])
        half = sb("half", [P, H])
        qs = [sb(f"qs{i}", [P, TILES, H, 2, D]) for i in range(2)]
        qst = [sb(f"qst{i}", [P, S]) for i in range(4)]
        pT = [sb(f"pT{i}", [P, 2, 4 * WIN - P]) for i in range(2)]
        oT = sb("oT", [P, PAIRS, S])
        dn = sb("dn", [P, S])
        yT = sb("yT", [P, S])
        hs1 = sb("hs1", [SH1, S])
        hs2 = sb("hs2", [SH2, S])
        he2 = sb("he2", [P, 2, S])
        ge = sb("ge", [P, 8, SLOTS, E])
        gcmp = sb("gcmp", [P, 3, SLOTS, E, E])
        gst = sb("gst", [P, 6, SLOTS])
        eo, eo2 = (oT[:, 2 * i:2 * i + 2, :].rearrange("p a (b e d) -> p (a b) e d", e=E, d=D) for i in range(2))
        he1 = oT[:, 4:8, :]
        fsum = sb("fsum", [P, 3, SLOTS, D])

        bank = [ctx.enter_context(nc.psum_tensor(f"bank{i}", [P, 512], FP32)) for i in range(8)]
        QP0, QP1, QT, OP, DN = bank[0], bank[1], bank[2], bank[6], bank[7]
        SC = bank[3:6]

        def ec(name):
            o, w = EARLY[name]
            return early[:, o:o + w]

        def lc(name, rows=P):
            o, w = LATE[name]
            return late[0:rows, o:o + w]

        def wc(name, rows=D):
            o, w = W64[name]
            return w64[0:rows, o:o + w]

        ident = ec("ident")

        s_idx = sem("s_idx")
        s_halo0 = [sem(f"s_halo0_{b}") for b in range(B)]
        s_emb = [sem(f"s_emb{b}") for b in range(B)]
        s_halo = [sem(f"s_halo{b}") for b in range(B)]
        s_early = sem("s_early")
        s_late = sem("s_late")
        s_w64 = sem("s_w64")
        s_ones = sem("s_ones")
        s_const = sem("s_const")
        s_shift = sem("s_shift")
        s_xn = sem("s_xn")
        s_xTp = sem("s_xTp")
        s_xT = sem("s_xT")
        s_kv = sem("s_kv")
        s_ktok = sem("s_ktok")
        s_kp = sem("s_kp")
        s_kst = sem("s_kst")
        s_v = sem("s_v")
        s_q = sem("s_q")
        s_qsq = sem("s_qsq")
        s_qs = sem("s_qs")
        s_qd = sem("s_qd")
        s_qt = sem("s_qt")
        s_qst = sem("s_qst")
        s_sc = sem("s_sc")
        s_p = sem("s_p")
        s_pv = sem("s_pv")
        s_oT = sem("s_oT")
        s_yTp = sem("s_yTp")
        s_yT = sem("s_yT")
        s_y = sem("s_y")
        s_h = sem("s_h")
        s_f1 = sem("s_f1")
        s_f1r = sem("s_f1r")
        s_f2 = sem("s_f2")
        s_f2r = sem("s_f2r")
        s_g = sem("s_g")
        s_gc = sem("s_gc")
        s_gx = sem("s_gx")
        s_ge = sem("s_ge")
        s_gp = sem("s_gp")
        s_gw = sem("s_gw")
        s_f3 = sem("s_f3")
        s_fin = sem("s_fin")
        s_out = sem("s_out")
        s_dve = sem("s_dve")
        s_half = sem("s_half")
        s_sum = sem("s_sum")
        s_root = sem("s_root")

        block = ctx.enter_context(nc.Block())

        HALVES = [[(0, 0, WIN), (1, WIN, WIN)], [(2, 0, WIN), (3, WIN, P)]]
        HALF_W = [2 * WIN, WIN + P]

        @block.sync
        def _(sp):
            sp.dma_start(idx[:, :], tok).then_inc(s_idx, 16)
            for b in range(B):
                sp.dma_start(emb[P - 1:P, b, SLOTS:, :],
                             table[0:1, :].unsqueeze(1).broadcast_to([1, SLOTS, C * D])).then_inc(s_halo0[b], 16)
            sp.dma_start(early[:, :], early_d).then_inc(s_early, 16)
            sp.dma_start(w64[0:D, :], w64_d).then_inc(s_w64, 16)
            for b in range(B):
                sp.wait_ge(s_emb[b], 16 * SLOTS)
                sp.dma_start(emb[0:P - 1, b, SLOTS:, :], emb[1:P, b, 0:SLOTS, :]).then_inc(s_halo[b], 16)
            for b in range(B):
                sp.wait_ge(s_fin, b + 1)
                sp.dma_start(out[b].rearrange("(p j) d -> p j d", j=SLOTS), h[:, b, :, :]).then_inc(s_out, 16)
            sp.wait_ge(s_out, 16 * B)

        @block.gpsimd
        def _(pool):
            pool.wait_ge(s_idx, 16)
            for b in range(B):
                for j in range(SLOTS):
                    pool.indirect_dma_start(
                        out=emb[:, b, j, :], out_offset=None, in_=table,
                        in_offset=bass.IndirectOffsetOnAxis(ap=idx[:, b * SLOTS + j:b * SLOTS + j + 1], axis=0),
                    ).then_inc(s_emb[b], 16)
            pool.memset(half[:, :], -0.5).then_inc(s_half, 1)
            pool.wait_ge(s_half, 1)
            pool.memset(ones[:, :], 1.0).then_inc(s_ones, 1)
            pool.wait_ge(s_ones, 1)
            pool.memset(xT[D:D + 1, :], 1.0).then_inc(s_ones, 1)
            pool.wait_ge(s_ones, 2)
            roots = [0]

            def root(out_, in_):
                roots[0] += 1
                pool.wait_ge(s_sum, roots[0])
                pool.tensor_tensor(out_, in_, half[:, 0:in_.shape[-1]], ALU.pow).then_inc(s_root, 1)

            for b in range(B):
                if b:
                    pool.wait_ge(s_qd, b * TILES)
                root(stat[:, 4, :], stat[:, 3, :])
                root(kstat[:, 2, :], kstat[:, 1, :])
                for t in range(TILES):
                    if t:
                        pool.wait_ge(s_qd, b * TILES + t)
                    root(qstat[:, 2, :], qstat[:, 1, :])
                    pool.wait_ge(s_qs, b * TILES + t + 1)
                    pool.tensor_copy(qs[b % 2][:, t, :, 1, :], qs[b % 2][:, t, :, 0, :]).then_inc(s_qd, 1)
            pool.wait_ge(s_qd, B * TILES)
            for b in range(B):
                root(stat[:, 4, :], stat[:, 3, :])

        @block.scalar
        def _(act):
            act.dma_start(mask[:, :], mask_d).then_inc(s_early, 16)
            act.dma_start(w64[D:D + 1, W64["gW"][0]:W64["gW"][0] + E], gb_d).then_inc(s_w64, 16)
            act.dma_start(late[:, :], late_d).then_inc(s_late, 16)
            act.wait_ge(s_early, 32)
            act.activation(identb[:, :], ident, ACT.Copy).then_inc(s_const, 1)

            def keep_xT(n):
                act.wait_ge(s_xTp, n + 1)
                if n == 0:
                    act.wait_ge(s_ones, 2)
                src = QP0[0:D, :]
                if n < B:
                    src = src.rearrange("d (j p) -> d p j", j=SLOTS)
                    act.activation(xT[0:D, :].rearrange("d (p j) -> d p j", j=SLOTS), src, ACT.Copy).then_inc(s_xT, 1)
                else:
                    act.activation(xT[0:D, :], src, ACT.Copy).then_inc(s_xT, 1)

            def square_q(b, t):
                n = b * TILES + t
                act.wait_ge(s_q, n + 1)
                if n:
                    act.wait_ge(s_qs, n)
                for i, bk in enumerate((QP0, QP1)):
                    act.activation(qsq[:, 8 * i:8 * i + 8, :], bk[:, :].rearrange("p (h d) -> p h d", d=D),
                                   ACT.Square).then_inc(s_qsq, 1)

            def keep_kst(b):
                act.wait_ge(s_kp, b + 1)
                act.activation(kst[:, :], QP0[:, :], ACT.Copy).then_inc(s_kst, 1)

            def slices(b, slot):
                if b < B:
                    if slot == 1:
                        keep_xT(b)
                    elif 3 <= slot <= 6:
                        square_q(b, slot - 3)
                    elif slot == 7:
                        keep_kst(b)

            for slot in range(8):
                slices(0, slot)
            act.wait_ge(s_shift, 1)
            for b in range(B):
                for p in range(PAIRS):
                    n = b * PAIRS + p
                    if n >= 2:
                        act.wait_ge(s_pv, n - 1)
                    for hh in range(2):
                        for half in range(2):
                            u = 4 * n + 2 * hh + half
                            act.wait_ge(s_sc, u + 1)
                            w = HALF_W[half]
                            act.activation(pT[n % 2][:, hh, 2 * WIN * half:2 * WIN * half + w],
                                           SC[u % 3][:, 0:w], ACT.Exp, bias=shift[:, 1:2]).then_inc(s_p, 1)
                    slices(b + 1, p)
                act.wait_ge(s_yTp, b + 1)
                if b:
                    act.wait_ge(s_y, b)
                act.activation(yT[:, :], OP[:, :], ACT.Copy).then_inc(s_yT, 1)

            act.wait_ge(s_late, 16)
            for b in range(B):
                keep_xT(B + b)
                act.wait_ge(s_gx, b + 1)
                act.activation(ge[:, 1], ge[:, 0], ACT.Exp).then_inc(s_ge, 1)
                act.wait_ge(s_gp, b + 1)
                act.activation(ge[:, 4], ge[:, 3], ACT.Exp).then_inc(s_gw, 1)
                for e in range(E):
                    act.wait_ge(s_f1, b * (E + 1) + e + 2)
                    if b:
                        act.wait_ge(s_f2, 3 * b)
                    act.activation(he1[:, e, :], bank[3 + e][:, :], ACT.Relu,
                                   bias=lc("eb1")[:, e:e + 1]).then_inc(s_f1r, 1)

        @block.vector
        def _(dve):
            links = [0]

            def link(ins):
                links[0] += 1
                ins.then_inc(s_dve, 1)
                dve.wait_ge(s_dve, links[0])

            roots = [0]

            def root(ins):
                roots[0] += 1
                ins.then_inc(s_sum, 1)
                dve.wait_ge(s_root, roots[0])

            def norm(src):
                link(dve.reduce_sum(stat[:, 0, :], src, AX.X))
                link(dve.tensor_scalar(stat[:, 1, :], stat[:, 0, :], 1.0 / D, None, ALU.mult))
                link(dve.tensor_tensor(xc[:, :, :], src, stat[:, 1, :].unsqueeze(2).broadcast_to([P, SLOTS, D]),
                                       ALU.subtract))
                link(dve.tensor_tensor(sq[:, :, :], xc[:, :, :], xc[:, :, :], ALU.mult))
                link(dve.reduce_sum(stat[:, 2, :], sq[:, :, :], AX.X))
                root(dve.tensor_scalar(stat[:, 3, :], stat[:, 2, :], D * LN_EPS, None, ALU.add))
                ins = dve.scalar_tensor_tensor(xn[:, :, :], xc[:, :, :], float(D) ** 0.5,
                                               stat[:, 4, :].unsqueeze(2).broadcast_to([P, SLOTS, D]),
                                               ALU.mult, ALU.mult)
                ins.then_inc(s_xn, 1)

            def embed(b):
                dve.wait_ge(s_emb[b], 16 * SLOTS)
                dve.wait_ge(s_halo[b], 16)
                dve.wait_ge(s_halo0[b], 16)
                if b:
                    dve.wait_ge(s_xTp, b)
                rows = emb[:, b, :, :].rearrange("p k c -> p (k c)")
                shifted = bass.AP(tensor=rows.tensor, offset=rows.offset,
                                  ap=[rows.ap[0], [C * D, SLOTS], [1, D], [C * D + D, C]])
                link(dve.reduce_sum(h[:, b, :, :], shifted, AX.X))
                norm(h[:, b, :, :])

            def keys(b):
                dve.wait_ge(s_kv, b + 1)
                kv = QP1[:, :].rearrange("p (t c) -> p t c", c=2 * D)
                k = kv[:, :, 0:D]
                if b:
                    dve.wait_ge(s_v, b)
                    dve.wait_ge(s_kp, b)
                link(dve.tensor_copy(v_next[:, :, :], kv[:, :, D:2 * D]))
                link(dve.tensor_copy(kq[:, 0], k))
                link(dve.tensor_tensor(kq[:, 1], kq[:, 0], kq[:, 0], ALU.mult))
                link(dve.reduce_sum(kstat[:, 0, :], kq[:, 1], AX.X))
                root(dve.tensor_scalar(kstat[:, 1, :], kstat[:, 0, :], D * RMS_EPS, None, ALU.add))
                link(dve.tensor_tensor(kq[:, 1], kq[:, 0], kstat[:, 2, :].unsqueeze(2).broadcast_to([P, TILES, D]),
                                       ALU.mult))
                cos = ec("k_cos").rearrange("p (t d) -> p t d", d=D)
                sin = ec("k_sin").rearrange("p (t d) -> p t d", d=D)
                link(dve.tensor_tensor(kq[:, 0], kq[:, 1], cos, ALU.mult))
                for e in range(2):
                    link(dve.tensor_tensor(kq[:, 2, :, e::2], kq[:, 1, :, 1 - e::2], sin[:, :, e::2], ALU.mult))
                link(dve.tensor_tensor(kq[:, 3], kq[:, 0], kq[:, 2], ALU.add))
                link(dve.tensor_tensor(ktok[:, :, 0, :], kq[:, 3], gs[:, :].unsqueeze(1).broadcast_to([P, TILES, D]),
                                       ALU.mult))
                sign = ec("swap_sign")
                for e in range(2):
                    ins = dve.tensor_tensor(ktok[:, :, 1, e::2], ktok[:, :, 0, 1 - e::2],
                                            sign[:, e::2].unsqueeze(1).broadcast_to([P, TILES, D // 2]), ALU.mult)
                    ins.then_inc(s_ktok, 1)

            def queries(b, t):
                n = b * TILES + t
                dve.wait_ge(s_qsq, 2 * n + 2)
                link(dve.reduce_sum(qstat[:, 0, :], qsq[:, :, :], AX.X))
                root(dve.tensor_scalar(qstat[:, 1, :], qstat[:, 0, :], D * RMS_EPS, None, ALU.add))
                if b >= 2:
                    dve.wait_ge(s_qt, (b - 1) * H)
                for i, bk in enumerate((QP0, QP1)):
                    ins = dve.tensor_tensor(qs[b % 2][:, t, 8 * i:8 * i + 8, 0, :],
                                            bk[:, :].rearrange("p (h d) -> p h d", d=D),
                                            qstat[:, 2, 8 * i:8 * i + 8].unsqueeze(2).broadcast_to([P, 8, D]),
                                            ALU.mult)
                    if i == 0:
                        link(ins)
                    else:
                        ins.then_inc(s_qs, 1)
                        dve.wait_ge(s_qs, n + 1)

            def slices(b, slot):
                if b < B:
                    if slot == 0:
                        embed(b)
                    elif slot == 2:
                        keys(b)
                    elif 3 <= slot <= 6:
                        queries(b, slot - 3)

            def rotate(n):
                dve.wait_ge(s_qt, n + 1)
                if n >= 4:
                    dve.wait_ge(s_sc, 2 * (n - 3))
                dve.tensor_tensor(qst[n % 4][:, :], QT[:, :], ec("trig"), ALU.mult).then_inc(s_qst, 1)

            def divide(n):
                dve.wait_ge(s_pv, n + 1)
                link(dve.reciprocal(dn[:, :], DN[:, :]))
                b = n // PAIRS
                if b:
                    dve.wait_ge(s_yTp, b)
                dve.tensor_tensor(oT[:, n % PAIRS, :], OP[:, :], dn[:, :], ALU.mult).then_inc(s_oT, 1)

            dve.wait_ge(s_early, 32)
            link(dve.tensor_tensor(gs[:, :], ec("qn"), ec("kn"), ALU.mult))
            link(dve.tensor_scalar(gs[:, :], gs[:, :], float(D) ** 0.5, None, ALU.mult))
            link(dve.tensor_scalar(sq[:, 1, :], gs[:, :], -1.0, None, ALU.mult))
            link(dve.tensor_tensor(sq[:, 0, :], gs[:, :], sq[:, 1, :], ALU.max))
            link(dve.reduce_max(shift[:, 0:1], sq[:, 0, :], AX.X))
            link(dve.tensor_scalar(shift[:, 1:2], shift[:, 0:1], -1.0, 80.0, ALU.mult, ALU.add))
            dve.tensor_scalar(shift[:, 1:2], shift[:, 1:2], 0.0, None, ALU.min).then_inc(s_shift, 1)
            for slot in range(8):
                slices(0, slot)
            rotate(0)
            rotate(1)
            for b in range(B):
                if b:
                    dve.wait_ge(s_pv, b * PAIRS)
                dve.tensor_copy(v[:, :, :], v_next[:, :, :]).then_inc(s_v, 1)
                for p in range(PAIRS):
                    n = b * PAIRS + p
                    if n + 1 < B * PAIRS:
                        if p < PAIRS - 1:
                            rotate(2 * n + 2)
                            rotate(2 * n + 3)
                    slices(b + 1, p)
                    if p:
                        divide(n - 1)
                if b + 1 < B:
                    rotate(2 * (b + 1) * PAIRS)
                    rotate(2 * (b + 1) * PAIRS + 1)
                divide(b * PAIRS + PAIRS - 1)
                dve.wait_ge(s_y, b + 1)
                dve.tensor_tensor(h[:, b, :, :], h[:, b, :, :], DN[:, 0:SLOTS * D].rearrange("p (j d) -> p j d", d=D),
                                  ALU.add).then_inc(s_h, 1)

            dve.wait_ge(s_late, 16)
            b3 = lc("eb3").rearrange("p (e d) -> p e d", d=D).unsqueeze(1).broadcast_to([P, SLOTS, E, D])
            sb3 = lc("sb3").unsqueeze(1).broadcast_to([P, SLOTS, D])
            before = lc("before").rearrange("p (e f) -> p e f", f=E)

            def per_e(x):
                return x.unsqueeze(2).broadcast_to([P, SLOTS, E])

            for b in range(B):
                dve.wait_ge(s_h, b + 1)
                dve.wait_ge(s_xTp, B + b)
                norm(h[:, b, :, :])
                dve.wait_ge(s_g, b + 1)
                if b:
                    dve.wait_ge(s_fin, b)
                logits = QP1[:, 0:SLOTS * E].rearrange("p (j e) -> p j e", e=E)
                link(dve.tensor_copy(ge[:, 7], logits))
                link(dve.reduce_max(gst[:, 0, :], ge[:, 7], AX.X))
                dve.tensor_tensor(ge[:, 0], ge[:, 7], per_e(gst[:, 0, :]), ALU.subtract).then_inc(s_gx, 1)
                dve.wait_ge(s_ge, b + 1)
                link(dve.reduce_sum(gst[:, 1, :], ge[:, 1], AX.X))
                link(dve.reciprocal(gst[:, 4, :], gst[:, 1, :]))
                link(dve.tensor_tensor(ge[:, 2], ge[:, 1], per_e(gst[:, 4, :]), ALU.mult))
                link(dve.reduce_max(gst[:, 2, :], ge[:, 2], AX.X))
                dve.tensor_tensor(ge[:, 3], ge[:, 2], per_e(gst[:, 2, :]), ALU.subtract).then_inc(s_gp, 1)
                for j in range(SLOTS):
                    mine = ge[:, 2, j].unsqueeze(2).broadcast_to([P, E, E])
                    other = ge[:, 2, j].unsqueeze(1).broadcast_to([P, E, E])
                    link(dve.tensor_tensor(gcmp[:, 0, j], other, mine, ALU.is_gt))
                    link(dve.tensor_tensor(gcmp[:, 1, j], other, mine, ALU.is_equal))
                link(dve.tensor_tensor(gcmp[:, 2], gcmp[:, 1], before.unsqueeze(1).broadcast_to([P, SLOTS, E, E]),
                                       ALU.mult))
                link(dve.tensor_tensor(gcmp[:, 1], gcmp[:, 0], gcmp[:, 2], ALU.add))
                link(dve.reduce_sum(ge[:, 5], gcmp[:, 1], AX.X))
                link(dve.tensor_scalar(ge[:, 6], ge[:, 5], 1.5, None, ALU.is_lt))
                dve.wait_ge(s_gw, b + 1)
                link(dve.tensor_tensor(ge[:, 5], ge[:, 4], ge[:, 6], ALU.mult))
                link(dve.reduce_sum(gst[:, 3, :], ge[:, 5], AX.X))
                link(dve.reciprocal(gst[:, 5, :], gst[:, 3, :]))
                link(dve.tensor_tensor(ge[:, 6], ge[:, 5], per_e(gst[:, 5, :]), ALU.mult))
                dve.wait_ge(s_f1, b * (E + 1) + 1)
                dve.tensor_scalar(hs1[:, :], bank[2][0:SH1, :], lc("sb1", SH1), 0.0, ALU.add, ALU.max).then_inc(s_f1r, 1)
                dve.wait_ge(s_f2, 3 * b + 1)
                dve.tensor_scalar(hs2[:, :], bank[0][:, :], lc("sb2"), 0.0, ALU.add, ALU.max).then_inc(s_f2r, 1)
                for i in range(2):
                    dve.wait_ge(s_f2, 3 * b + 2 + i)
                    dve.tensor_scalar(he2[:, i, :], bank[(7, 2)[i]][:, :], lc("eb2")[:, i:i + 1], 0.0,
                                      ALU.add, ALU.max).then_inc(s_f2r, 1)
                dve.wait_ge(s_f3, b + 1)
                for i in range(2):
                    link(dve.tensor_tensor(
                        eo[:, :, 2 * i:2 * i + 2, :], bank[3 + i][:, :].rearrange("p (j e d) -> p j e d", e=2, d=D),
                        b3[:, :, 2 * i:2 * i + 2, :], ALU.add))
                link(dve.tensor_tensor(eo2[:, :, :, :], eo[:, :, :, :],
                                       ge[:, 6].unsqueeze(3).broadcast_to([P, SLOTS, E, D]), ALU.mult))
                link(dve.reduce_sum(fsum[:, 0], eo2[:, :, :, :].rearrange("p j e d -> p j d e"), AX.X))
                link(dve.tensor_tensor(fsum[:, 1], bank[5][:, 0:SLOTS * D].rearrange("p (j d) -> p j d", d=D), sb3,
                                       ALU.add))
                link(dve.tensor_tensor(fsum[:, 2], fsum[:, 0], fsum[:, 1], ALU.add))
                dve.tensor_tensor(h[:, b, :, :], h[:, b, :, :], fsum[:, 2], ALU.add).then_inc(s_fin, 1)

        @block.tensor
        def _(pe):
            def transpose_x(n):
                pe.wait_ge(s_xn, n + 1)
                if n == 0:
                    pe.wait_ge(s_early, 32)
                elif n < B:
                    pe.wait_ge(s_kst, n)
                elif n == B:
                    pe.wait_ge(s_qs, B * TILES)
                    pe.wait_ge(s_kst, B)
                else:
                    pe.wait_ge(s_f2r, 3 * (n - B) - 2)
                for j in range(SLOTS):
                    last = pe.transpose(QP0[0:D, j * P:(j + 1) * P], xn[:, j, :], ident)
                last.then_inc(s_xTp, 1)

            def project_kv(b):
                pe.wait_ge(s_xT, b + 1)
                pe.wait_ge(s_w64, 32)
                if b:
                    pe.wait_ge(s_qs, b * TILES)
                for t in range(TILES):
                    last = pe.matmul(QP1[:, t * 2 * D:(t + 1) * 2 * D], xT[0:D, t * P:(t + 1) * P], wc("wkv"),
                                     start=True, stop=True)
                last.then_inc(s_kv, 1)

            def project_q(b, t):
                if t:
                    pe.wait_ge(s_qs, b * TILES + t)
                else:
                    pe.wait_ge(s_ktok, 2 * b + 2)
                for i, bk in enumerate((QP0, QP1)):
                    last = pe.matmul(bk[:, :], xT[0:D, t * P:(t + 1) * P], wc("wq")[:, 512 * i:512 * i + 512],
                                     start=True, stop=True)
                last.then_inc(s_q, 1)

            def transpose_k(b):
                pe.wait_ge(s_qs, (b + 1) * TILES)
                if b:
                    pe.wait_ge(s_sc, 4 * b * PAIRS)
                for t in range(TILES):
                    last = pe.transpose(QP0[:, t * P:(t + 1) * P], ktok[:, t].rearrange("p a d -> p (a d)"), ident)
                last.then_inc(s_kp, 1)

            def slices(b, slot):
                if b < B:
                    if slot == 1:
                        transpose_x(b)
                    elif slot == 2:
                        project_kv(b)
                    elif 3 <= slot <= 6:
                        project_q(b, slot - 3)
                    elif slot == 7:
                        transpose_k(b)

            def transpose_q(n):
                b, head = n // H, n % H
                if head == 0:
                    pe.wait_ge(s_qd, (b + 1) * TILES)
                if n:
                    pe.wait_ge(s_qst, n)
                for t in range(TILES):
                    src = qs[b % 2][:, t, head].rearrange("p a d -> p (a d)")
                    last = pe.transpose(QT[:, t * P:(t + 1) * P], src, ident)
                last.then_inc(s_qt, 1)

            def scores(n):
                if n % H == 0:
                    pe.wait_ge(s_kst, n // H + 1)
                pe.wait_ge(s_qst, n + 1)
                for half in range(2):
                    u = 2 * n + half
                    if u >= 3:
                        pe.wait_ge(s_p, u - 2)
                    bk = SC[u % 3]
                    pe.matmul(bk[:, 0:HALF_W[half]], identb[:, :], mask[:, 0:HALF_W[half]], start=True, stop=False,
                              skip_group_check=True)
                    for kt, c, w in HALVES[half]:
                        last = pe.matmul(bk[:, c:c + w], kst[:, kt * P:(kt + 1) * P],
                                         qst[n % 4][:, kt * P:kt * P + w], start=False, stop=True,
                                         skip_group_check=True)
                    last.then_inc(s_sc, 1)

            def weigh(n):
                pe.wait_ge(s_p, 4 * n + 4)
                if n:
                    pe.wait_ge(s_oT, n)
                if n % PAIRS == 0:
                    pe.wait_ge(s_v, n // PAIRS + 1)
                    if n:
                        pe.wait_ge(s_h, n // PAIRS)
                for bk, ones_ in ((OP, False), (DN, True)):
                    for t in range(TILES):
                        w = WIN if t < TILES - 1 else P
                        for hh in range(2):
                            last = pe.matmul(bk[D * hh:D * hh + D, t * P:t * P + w],
                                             ones[:, :] if ones_ else v[:, t, :],
                                             pT[n % 2][:, hh, t * WIN:t * WIN + w],
                                             start=(t == 0), stop=(t == TILES - 1), skip_group_check=True)
                last.then_inc(s_pv, 1)

            for slot in range(8):
                slices(0, slot)
            transpose_q(0)
            transpose_q(1)
            pe.wait_ge(s_const, 1)
            pe.wait_ge(s_ones, 2)
            for b in range(B):
                for p in range(PAIRS):
                    n = b * PAIRS + p
                    scores(2 * n)
                    if p < PAIRS - 1:
                        transpose_q(2 * n + 2)
                    scores(2 * n + 1)
                    if p < PAIRS - 1:
                        transpose_q(2 * n + 3)
                    slices(b + 1, p)
                    if p:
                        weigh(n - 1)
                if b + 1 < B:
                    transpose_q(2 * n + 2)
                    transpose_q(2 * n + 3)
                weigh(n)
                if b == 0:
                    pe.wait_ge(s_late, 16)
                pe.wait_ge(s_oT, (b + 1) * PAIRS)
                for q in range(PAIRS // 2):
                    for odd in range(2):
                        p = 2 * q + odd
                        last = pe.matmul(OP[D * odd:D * odd + D, :], lc("wo")[:, p * D:(p + 1) * D], oT[:, p, :],
                                         start=(q == 0), stop=(q == PAIRS // 2 - 1), skip_group_check=True)
                last.then_inc(s_yTp, 1)
                pe.wait_ge(s_yT, b + 1)
                yv = yT[:, :].rearrange("d (p j) -> d j p", j=SLOTS)
                for j in range(SLOTS):
                    last = pe.matmul(DN[:, j * D:(j + 1) * D], yv[:, j, :], ec("ident2"), start=True, stop=True)
                last.then_inc(s_y, 1)

            for b in range(B):
                transpose_x(B + b)
                pe.wait_ge(s_xT, B + b + 1)
                if b:
                    pe.wait_ge(s_gp, b)
                for j in range(SLOTS):
                    last = pe.matmul(QP1[:, j * E:(j + 1) * E], xT[:, j * P:(j + 1) * P], wc("gW", D + 1),
                                     start=True, stop=True)
                last.then_inc(s_g, 1)
                if b:
                    pe.wait_ge(s_fin, b)
                pe.matmul(bank[2][0:SH1, :], wc("sW1"), xT[0:D, :], start=True, stop=True).then_inc(s_f1, 1)
                for e in range(E):
                    pe.matmul(bank[3 + e][:, :], wc("eW1")[:, e * EH1:(e + 1) * EH1], xT[0:D, :],
                              start=True, stop=True).then_inc(s_f1, 1)
                pe.wait_ge(s_f1r, (E + 1) * b + E + 1)
                pe.matmul(bank[0][:, :], wc("sW2", SH1), hs1[:, :], start=True, stop=True).then_inc(s_f2, 1)
                for i in range(2):
                    for k in range(2):
                        e = 2 * i + k
                        last = pe.matmul(bank[(7, 2)[i]][D * k:D * k + D, :], lc("eW2")[:, e * EH2:(e + 1) * EH2],
                                         he1[:, e, :], start=True, stop=True)
                    last.then_inc(s_f2, 1)
                pe.wait_ge(s_f2r, 3 * b + 3)
                for i in range(2):
                    for j in range(SLOTS):
                        pe.matmul(bank[3 + i][:, j * P:(j + 1) * P], he2[:, i, j * P:(j + 1) * P],
                                  lc("eW3")[:, i * P:(i + 1) * P], start=True, stop=True)
                for j in range(SLOTS):
                    last = pe.matmul(bank[5][:, j * D:(j + 1) * D], hs2[:, j * P:(j + 1) * P], lc("sW3"),
                                     start=True, stop=True)
                last.then_inc(s_f3, 1)


def _tables():
    f32 = np.float32
    freqs = np.power(f32(10000.0), (f32(-2.0) * np.arange(D // 2, dtype=f32) / f32(D)).astype(f32)).astype(f32)
    theta = (np.arange(S, dtype=f32)[:, None] * freqs[None, :]).astype(f32)
    cos, sin = np.repeat(np.cos(theta), 2, 1), np.repeat(np.sin(theta), 2, 1)
    sign = np.tile(np.array([-1.0, 1.0], f32), D // 2)
    by_tile = lambda a: a.reshape(TILES, P, D).transpose(1, 0, 2).reshape(P, TILES * D)
    key, query = np.arange(P)[:, None], np.arange(P)[None, :]
    own, after = np.where(key <= query, 0.0, NEG), np.where(query <= key, 0.0, NEG)
    e = np.arange(E)
    return {
        "ident": np.eye(P, dtype=f32), "trig": np.concatenate([cos.T, sin.T], 0),
        "k_cos": by_tile(cos), "k_sin": by_tile(sin * sign),
        "swap_sign": np.tile(-sign, (P, 1)), "ident2": np.tile(np.eye(D, dtype=f32), (2, 1)),
        "mask": np.concatenate([own, after, own, after], 1).astype(f32),
        "before": np.tile((e[None, :] < e[:, None]).astype(f32).reshape(1, E * E), (P, 1)),
    }


def _pack(where, width, rows, parts):
    a = np.zeros((rows, width), np.float32)
    for name, part in parts.items():
        o, w = where[name]
        assert part.shape[1] == w, name
        a[:part.shape[0], o:o + w] = part
    return a


def kernel(**inputs):
    import ml_dtypes
    import concourse.bacc as bacc
    from concourse.bass_utils import run_bass_kernel_spmd

    i = {k.replace("L0_", ""): np.asarray(a) for k, a in inputs.items()}
    t = _tables()
    rows = lambda a: np.tile(a.reshape(1, -1), (P, 1))
    early = _pack(EARLY, EARLY_W, P, {**{k: t[k] for k in ("ident", "trig", "k_cos", "k_sin", "swap_sign", "ident2")},
                                      "qn": rows(i["attn_q_norm_w"]), "kn": rows(i["attn_k_norm_w"])})
    eW3 = np.zeros((P, 2, 2, D), np.float32)
    for e in range(E):
        eW3[D * (e % 2):D * (e % 2) + D, e // 2, e % 2] = i["ffn_eW3"][e]
    late = _pack(LATE, LATE_W, P, {
        "wo": i["attn_wo"].T.reshape(PAIRS, P, D).transpose(1, 0, 2).reshape(P, -1),
        "eW2": i["ffn_eW2"].transpose(1, 0, 2).reshape(EH1, -1), "sW3": i["ffn_sW3"], "eW3": eW3.reshape(P, -1),
        "eb1": i["ffn_eb1"].T, "eb2": i["ffn_eb2"].reshape(2, P).T, "sb2": i["ffn_sb2"].reshape(-1, 1),
        "sb1": i["ffn_sb1"].reshape(-1, 1), "eb3": rows(i["ffn_eb3"]), "sb3": rows(i["ffn_sb3"]),
        "before": t["before"]})
    w64 = _pack(W64, W64_W, D, {
        "wq": i["attn_wq"].T, "wkv": i["attn_wkv"].T, "sW1": i["ffn_sW1"],
        "eW1": i["ffn_eW1"].transpose(1, 0, 2).reshape(D, -1), "sW2": i["ffn_sW2"], "gW": i["ffn_gW"]})
    arrays = {
        "tok": np.ascontiguousarray(i["x"].reshape(B, P, SLOTS).transpose(1, 0, 2).reshape(P, B * SLOTS)),
        "table": np.ascontiguousarray(i["tok_emb_table"].reshape(-1, C * D)),
        "early": early, "mask": t["mask"].astype(ml_dtypes.bfloat16), "late": late, "w64": w64,
        "gb": np.ascontiguousarray(i["ffn_gb"].reshape(1, E)),
    }
    nc = bacc.Bacc("TRN2", target_bir_lowering=False, num_devices=1)
    aps = [nc.dram_tensor("in_" + n, a.shape, mybir.dt.from_np(a.dtype), kind="ExternalInput").ap()
           for n, a in arrays.items()]
    out = nc.dram_tensor("out_h", (B, S, D), FP32, kind="ExternalOutput").ap()
    build(nc, *aps, out)
    r = run_bass_kernel_spmd(nc, [{"in_" + n: a for n, a in arrays.items()}], core_ids=[0])
    return r.results[0]["out_h"]
```

```python
import concourse.bass as bass
import concourse.mybir as mybir
import numpy as np
from contextlib import ExitStack

FP32 = mybir.dt.float32
I32 = mybir.dt.int32
ALU = mybir.AluOpType
ACT = mybir.ActivationFunctionType
AX = mybir.AxisListType

B, S, D = 4, 512, 64
C = 5
H = 16
PAIRS = H // 2
P = 128
TILES = S // P
SLOTS = S // P
WIN = 2 * P
E, EH1, EH2, SH1, SH2 = 4, 128, 64, 64, 128
LN_EPS, RMS_EPS = 1e-5, 1.1920929e-07

def _columns(parts):
    at, where = 0, {}
    for name, width in parts:
        where[name] = (at, width)
        at += width
    return where, at

EARLY, EARLY_W = _columns([("ident", P), ("trig", S), ("k_cos", TILES * D), ("k_sin", TILES * D),
                           ("swap_sign", D), ("qn", D), ("kn", D), ("ident2", D)])
LATE, LATE_W = _columns([("wo", PAIRS * D), ("eW2", E * EH2), ("sW3", D), ("eW3", 2 * P), ("eb1", E),
                         ("eb2", 2), ("sb2", 1), ("sb1", 1), ("eb3", E * D), ("sb3", D), ("before", E * E)])
W64, W64_W = _columns([("wq", H * D), ("wkv", 2 * D), ("sW1", SH1), ("eW1", E * EH1), ("sW2", SH2), ("gW", E)])


def build(nc, tok, table, early_d, late_d, w64_d, gb_d, out):
    with ExitStack() as ctx:
        def sb(name, shape, dt=FP32):
            return ctx.enter_context(nc.sbuf_tensor(name, shape, dt))

        def sem(name):
            return ctx.enter_context(nc.semaphore(name))

        idx = sb("idx", [P, B * SLOTS], I32)
        emb = sb("emb", [P, B, 2 * SLOTS, C * D])
        early = sb("early", [P, EARLY_W])
        late = sb("late", [P, LATE_W])
        w64 = sb("w64", [D + 1, W64_W])
        ones = sb("ones", [P, D])
        gs = sb("gs", [P, D])
        shift = sb("shift", [P, 2])
        h = sb("h", [P, B, SLOTS, D])
        xc = sb("xc", [P, SLOTS, D])
        sq = sb("sq", [P, SLOTS, D])
        xn = sb("xn", [P, SLOTS, D])
        stat = sb("stat", [P, 8, SLOTS])
        xT = sb("xT", [D + 1, S])
        kq = sb("kq", [P, 4, TILES, D])
        kstat = sb("kstat", [P, 5, TILES])
        ktok = sb("ktok", [P, TILES, 2, D])
        kst = [sb(f"kst{i}", [P, S]) for i in range(2)]
        v = [sb(f"v{i}", [P, TILES, D]) for i in range(2)]
        qsq = [sb(f"qsq{i}", [P, H, D]) for i in range(2)]
        qstat = [sb(f"qstat{i}", [P, 5, H]) for i in range(2)]
        qs = [sb(f"qs{i}", [P, TILES, H, 2, D]) for i in range(2)]
        qst = [sb(f"qst{i}", [P, S]) for i in range(4)]
        pT = [sb(f"pT{i}", [P, 2, 4 * WIN - P]) for i in range(2)]
        pS = [sb(f"pS{i}", [P, 2, TILES - 1, P]) for i in range(2)]
        oT = sb("oT", [P, PAIRS, S])
        ln_dn = sb("ln_dn", [P, S])
        r0 = sb("r0", [P, S])
        nw = sb("nw", [P, 2, S])
        yT = sb("yT", [P, S])
        def reuse(b, at, width):
            return emb[:, b, :, :].rearrange("p k c -> p (k c)")[:, at:at + width]

        hs1 = reuse(0, 0, S)[0:SH1, :]
        hs2 = reuse(0, S, S)
        he2 = reuse(0, 2 * S, 2 * S).rearrange("p (i s) -> p i s", s=S)
        wb = reuse(1, 0, SLOTS * E * D).rearrange("p (j e d) -> p j e d", e=E, d=D)
        base = reuse(1, SLOTS * E * D, 5 * SLOTS * D).rearrange("p (i j d) -> p i j d", i=5, d=D)
        ge = sb("ge", [P, 8, SLOTS, E])
        gw = [sb(f"gw{i}", [P, SLOTS, E]) for i in range(2)]
        gcmp = reuse(3, 0, 3 * SLOTS * E * E).rearrange("p (i j e f) -> p i j e f", i=3, j=SLOTS, e=E)
        gst = sb("gst", [P, 6, SLOTS])
        eo2 = oT[:, 0:2, :].rearrange("p a (b e d) -> p (a b) e d", e=E, d=D)
        he1 = oT[:, 4:8, :]
        fsum = reuse(2, 0, 2 * SLOTS * D).rearrange("p (i j d) -> p i j d", i=2, d=D)

        bank = [ctx.enter_context(nc.psum_tensor(f"bank{i}", [P, 512], FP32)) for i in range(8)]
        QP0, QP1, QT, OP, DN = bank[0], bank[1], bank[2], bank[6], bank[7]
        SC = bank[3:6]
        L1, L2, L3 = bank[1:4], bank[4], bank[5:8]

        def q_banks(b, t):
            return [(bank[0], bank[1]), (bank[3], bank[4]), (bank[5], bank[6]), (bank[7], bank[2])][t if b == 0 else 0]

        def ec(name):
            o, w = EARLY[name]
            return early[:, o:o + w]

        def lc(name, rows=P):
            o, w = LATE[name]
            return late[0:rows, o:o + w]

        def wc(name, rows=D):
            o, w = W64[name]
            return w64[0:rows, o:o + w]

        ident = ec("ident")

        s_idx = sem("s_idx")
        s_halo0 = [sem(f"s_halo0_{b}") for b in range(B)]
        s_emb = [sem(f"s_emb{b}") for b in range(B)]
        s_halo = [sem(f"s_halo{b}") for b in range(B)]
        s_early = sem("s_early")
        s_late = sem("s_late")
        s_w64 = sem("s_w64")
        s_ones = sem("s_ones")
        s_shift = sem("s_shift")
        s_xn = sem("s_xn")
        s_xTp = sem("s_xTp")
        s_xT = sem("s_xT")
        s_kv = sem("s_kv")
        s_kv_read = sem("s_kv_read")
        s_krot = sem("s_krot")
        s_ktok = sem("s_ktok")
        s_kp = sem("s_kp")
        s_kst = sem("s_kst")
        s_q = sem("s_q")
        s_qsq = sem("s_qsq")
        s_qs = sem("s_qs")
        s_qd = sem("s_qd")
        s_qt = sem("s_qt")
        s_qst = sem("s_qst")
        s_sc = sem("s_sc")
        s_p = sem("s_p")
        s_pv = sem("s_pv")
        s_m = sem("s_m")
        s_ps = sem("s_ps")
        s_ln = sem("s_ln")
        s_r0 = sem("s_r0")
        s_qsum = sem("s_qsum")
        s_oT = sem("s_oT")
        s_yTp = sem("s_yTp")
        s_yT = sem("s_yT")
        s_y = sem("s_y")
        s_h = sem("s_h")
        s_f1 = sem("s_f1")
        s_f1r = sem("s_f1r")
        s_f2 = sem("s_f2")
        s_f2r = sem("s_f2r")
        s_g = sem("s_g")
        s_gc = sem("s_gc")
        s_gx = sem("s_gx")
        s_ge = sem("s_ge")
        s_gp = sem("s_gp")
        s_gw = sem("s_gw")
        s_gwt = sem("s_gwt")
        s_base = sem("s_base")
        s_f3 = sem("s_f3")
        s_l3 = sem("s_l3")
        s_fin = sem("s_fin")
        s_out = sem("s_out")
        s_dve = sem("s_dve")
        s_sum = sem("s_sum")
        s_log = sem("s_log")
        s_root = sem("s_root")

        block = ctx.enter_context(nc.Block())

        HALVES = [[(0, 0, WIN), (1, WIN, WIN)], [(2, 0, WIN), (3, WIN, P)]]
        HALF_W = [2 * WIN, WIN + P]

        @block.sync
        def _(sp):
            sp.dma_start(idx[:, :], tok).then_inc(s_idx, 16)
            for b in range(B):
                sp.dma_start(emb[P - 1:P, b, SLOTS:, :],
                             table[0:1, :].unsqueeze(1).broadcast_to([1, SLOTS, C * D])).then_inc(s_halo0[b], 16)
            sp.dma_start(early[:, :], early_d).then_inc(s_early, 16)
            sp.dma_start(w64[0:D, :], w64_d).then_inc(s_w64, 16)
            for b in range(B):
                sp.wait_ge(s_emb[b], 16 * SLOTS)
                sp.dma_start(emb[0:P - 1, b, SLOTS:, :], emb[1:P, b, 0:SLOTS, :]).then_inc(s_halo[b], 16)
            for b in range(B):
                sp.wait_ge(s_fin, b + 1)
                sp.dma_start(out[b].rearrange("(p j) d -> p j d", j=SLOTS), h[:, b, :, :]).then_inc(s_out, 16)
            sp.wait_ge(s_out, 16 * B)

        @block.gpsimd
        def _(pool):
            pool.memset(ones[:, :], 1.0).then_inc(s_ones, 1)
            pool.wait_ge(s_ones, 1)
            pool.memset(xT[D:D + 1, :], 1.0).then_inc(s_ones, 1)
            pool.wait_ge(s_ones, 2)
            pool.wait_ge(s_idx, 16)
            for b in range(B):
                for j in range(SLOTS):
                    pool.indirect_dma_start(
                        out=emb[:, b, j, :], out_offset=None, in_=table,
                        in_offset=bass.IndirectOffsetOnAxis(ap=idx[:, b * SLOTS + j:b * SLOTS + j + 1], axis=0),
                    ).then_inc(s_emb[b], 16)

            def strided(first, step, count):
                return bass.AP(tensor=first.tensor, offset=first.offset,
                               ap=[first.ap[0], [step, count], first.ap[-1]])

            def mask(n):
                own = pT[n % 2][:, :, 0:(TILES - 1) * WIN].rearrange("p h (t w) -> p h t w", w=WIN)
                for hh in range(2):
                    pool.wait_ge(s_p, 4 * n + 2 * hh + 2)
                    blocks = strided(pT[n % 2][:, hh, 0:P], WIN, TILES)
                    pool.affine_select(out=blocks, in_=blocks, compare_op=ALU.is_ge, fill=0.0, base=0,
                                       pattern=[[0, TILES], [1, P]], channel_multiplier=-1).then_inc(s_m, 1)
                    pool.wait_ge(s_m, 4 * n + 2 * hh + 1)
                    blocks = own[:, hh, :, P:WIN]
                    pool.affine_select(out=blocks, in_=blocks, compare_op=ALU.is_ge, fill=0.0, base=0,
                                       pattern=[[0, TILES - 1], [-1, P]], channel_multiplier=1).then_inc(s_m, 1)
                    pool.wait_ge(s_m, 4 * n + 2 * hh + 2)
                    if n >= 2:
                        pool.wait_ge(s_pv, n - 1)
                    nxt = strided(pT[n % 2][:, hh, WIN:WIN + P], WIN, TILES - 1)
                    pool.tensor_tensor(pS[n % 2][:, hh], nxt, own[:, hh, :, P:WIN], ALU.add).then_inc(s_ps, 1)
                    pool.wait_ge(s_ps, 2 * n + hh + 1)

            for n in range(B * PAIRS):
                mask(n)
            for b in range(B):
                pool.wait_ge(s_gwt, b + 1)
                if b:
                    pool.wait_ge(s_fin, b)
                step = s_base
                weight = gw[b % 2][:, :, :].unsqueeze(3).broadcast_to([P, SLOTS, E, D])
                b3 = lc("eb3").rearrange("p (e d) -> p e d", d=D).unsqueeze(1).broadcast_to([P, SLOTS, E, D])
                sb3 = lc("sb3").unsqueeze(1).broadcast_to([P, SLOTS, D])
                pool.tensor_tensor(wb[:, :, :, :], weight, b3, ALU.mult).then_inc(step, 1)
                pool.wait_ge(step, 6 * b + 1)
                for i, (o, x, y) in enumerate([
                        (0, wb[:, :, 0, :], wb[:, :, 1, :]), (1, wb[:, :, 2, :], wb[:, :, 3, :]),
                        (2, base[:, 0], base[:, 1]), (3, base[:, 2], sb3), (4, base[:, 3], h[:, b, :, :])]):
                    pool.tensor_tensor(base[:, o], x, y, ALU.add).then_inc(step, 1)
                    pool.wait_ge(step, 6 * b + 2 + i)

        @block.scalar
        def _(act):
            act.preload_act_table_set("natural_log_exp_and_others")
            act.dma_start(w64[D:D + 1, W64["gW"][0]:W64["gW"][0] + E], gb_d).then_inc(s_w64, 16)
            act.dma_start(late[:, :], late_d).then_inc(s_late, 16)

            def keep_xT(n):
                act.wait_ge(s_xTp, n + 1)
                if n == 0:
                    act.wait_ge(s_ones, 2)
                src = QP0[0:D, :]
                if n < B:
                    src = src.rearrange("d (j p) -> d p j", j=SLOTS)
                    act.activation(xT[0:D, :].rearrange("d (p j) -> d p j", j=SLOTS), src, ACT.Copy).then_inc(s_xT, 1)
                else:
                    act.activation(xT[0:D, :], src, ACT.Copy).then_inc(s_xT, 1)

            def square_q(b, t):
                n = b * TILES + t
                act.wait_ge(s_q, n + 1)
                if n >= 2:
                    act.wait_ge(s_qsum, n - 1)
                for i, bk in enumerate(q_banks(b, t)):
                    act.activation(qsq[t % 2][:, 8 * i:8 * i + 8, :], bk[:, :].rearrange("p (h d) -> p h d", d=D),
                                   ACT.Square).then_inc(s_qsq, 1)

            def copy_q(b, t):
                act.wait_ge(s_qs, b * TILES + t + 1)
                act.activation(qs[b % 2][:, t, :, 1, :], qs[b % 2][:, t, :, 0, :], ACT.Copy).then_inc(s_qd, 1)

            def keep_kst(b):
                act.wait_ge(s_kp, b + 1)
                act.activation(kst[b % 2][:, :], QP0[:, :], ACT.Copy).then_inc(s_kst, 1)

            roots = [0]

            def root(st):
                roots[0] += 1
                act.wait_ge(s_sum, roots[0])
                act.activation(st[:, 3, :], st[:, 1, :], ACT.Ln).then_inc(s_log, 1)
                act.wait_ge(s_log, roots[0])
                act.activation(st[:, 2, :], st[:, 3, :], ACT.Exp, scale=-0.5).then_inc(s_root, 1)

            def inverse_roots(b, slot):
                if slot == 7 and b + 1 < B:
                    root(stat)
                if b < B:
                    if slot == 1:
                        root(kstat)
                    elif 3 <= slot <= 6:
                        root(qstat[(slot - 3) % 2])

            def end(b, slot):
                if b < B:
                    if slot == 0:
                        keep_xT(b)
                    if 3 <= slot <= 6:
                        copy_q(b, slot - 3)
                    if 2 <= slot <= 5:
                        square_q(b, slot - 2)
                    elif slot == 6:
                        keep_kst(b)

            def near_reciprocal(n):
                act.wait_ge(s_pv, n + 1)
                act.activation(ln_dn[:, :], DN[:, :], ACT.Ln).then_inc(s_ln, 1)
                act.wait_ge(s_ln, n + 1)
                if n:
                    act.wait_ge(s_oT, n)
                act.activation(r0[:, :], ln_dn[:, :], ACT.Exp, scale=-1.0).then_inc(s_r0, 1)

            def keep_yT(b):
                act.wait_ge(s_yTp, b + 1)
                if b:
                    act.wait_ge(s_y, b)
                act.activation(yT[:, :], QP1[:, :], ACT.Copy).then_inc(s_yT, 1)

            root(stat)
            keep_xT(0)
            root(kstat)
            root(stat)
            square_q(0, 0)
            for t in range(TILES):
                if t + 1 < TILES:
                    square_q(0, t + 1)
                root(qstat[t % 2])
                if t:
                    copy_q(0, t - 1)
            copy_q(0, TILES - 1)
            keep_kst(0)
            act.wait_ge(s_shift, 1)

            def exps(n, hh):
                for half in range(2):
                    u = 4 * n + 2 * hh + half
                    act.wait_ge(s_sc, u + 1)
                    w = HALF_W[half]
                    act.activation(pT[n % 2][:, hh, 2 * WIN * half:2 * WIN * half + w],
                                   SC[u % 3][:, 0:w], ACT.Exp, bias=shift[:, 1:2]).then_inc(s_p, 1)

            for b in range(B):
                for p in range(PAIRS):
                    n = b * PAIRS + p
                    if n >= 2:
                        act.wait_ge(s_pv, n - 1)
                    exps(n, 0)
                    if p == 1 and b:
                        keep_yT(b - 1)
                    exps(n, 1)
                    inverse_roots(b + 1, p)
                    if n:
                        near_reciprocal(n - 1)
                    end(b + 1, p)
            near_reciprocal(B * PAIRS - 1)
            keep_yT(B - 1)

            act.wait_ge(s_late, 16)
            for b in range(B):
                if b == 0:
                    root(stat)
                    keep_xT(B)

                def first(i):
                    n = (E + 1) * b + i
                    act.wait_ge(s_f1, n + 1)
                    if b:
                        act.wait_ge(s_f2, 3 * b)
                    dst = hs1[:, :] if i == 0 else he1[:, i - 1, :]
                    rows = SH1 if i == 0 else EH1
                    act.activation(dst, L1[n % 3][0:rows, :], ACT.Relu,
                                   bias=lc("sb1", SH1) if i == 0 else lc("eb1")[:, i - 1:i]).then_inc(s_f1r, 1)

                def second(i):
                    act.wait_ge(s_f2, 3 * b + i + 1)
                    if b:
                        act.wait_ge(s_f3, 3 * (b - 1) + (1, 2, 3)[i])
                    act.activation(hs2[:, :] if i == 0 else he2[:, i - 1, :], L2[:, :], ACT.Relu,
                                   bias=lc("sb2") if i == 0 else lc("eb2")[:, i - 1:i]).then_inc(s_f2r, 1)

                first(0)
                first(1)
                act.wait_ge(s_gx, b + 1)
                act.activation(ge[:, 1], ge[:, 0], ACT.Exp).then_inc(s_ge, 1)
                if b + 1 < B:
                    root(stat)
                first(2)
                second(0)
                first(3)
                act.wait_ge(s_gp, b + 1)
                act.activation(ge[:, 4], ge[:, 3], ACT.Exp).then_inc(s_gw, 1)
                second(1)
                first(4)
                if b + 1 < B:
                    keep_xT(B + b + 1)
                second(2)

        @block.vector
        def _(dve):
            links, roots = [0], [0]

            def link(ins):
                links[0] += 1
                ins.then_inc(s_dve, 1)
                dve.wait_ge(s_dve, links[0])

            def ask_root(ins):
                roots[0] += 1
                ins.then_inc(s_sum, 1)
                return roots[0]

            def spread(x, n):
                return x.unsqueeze(2).broadcast_to([P, x.shape[-1], n])

            def norm_sums(src):
                link(dve.reduce_sum(stat[:, 5, :], src, AX.X))
                link(dve.tensor_scalar(stat[:, 6, :], stat[:, 5, :], 1.0 / D, None, ALU.mult))
                link(dve.tensor_tensor(xc[:, :, :], src, spread(stat[:, 6, :], D), ALU.subtract))
                link(dve.tensor_tensor(sq[:, :, :], xc[:, :, :], xc[:, :, :], ALU.mult))
                link(dve.reduce_sum(stat[:, 0, :], sq[:, :, :], AX.X))
                return ask_root(dve.tensor_scalar(stat[:, 1, :], stat[:, 0, :], D * LN_EPS, None, ALU.add))

            def refine(asked, st):
                dve.wait_ge(s_root, asked)
                link(dve.tensor_tensor(st[:, 0, :], st[:, 2, :], st[:, 2, :], ALU.mult))
                link(dve.tensor_tensor(st[:, 0, :], st[:, 0, :], st[:, 1, :], ALU.mult))
                link(dve.scalar_tensor_tensor(st[:, 4, :], st[:, 0, :], 3.0, st[:, 2, :], ALU.subtract, ALU.mult))

            def norm_scale(asked, n):
                refine(asked, stat)
                if n:
                    dve.wait_ge(s_xTp, n)
                dve.scalar_tensor_tensor(xn[:, :, :], xc[:, :, :], -0.5 * float(D) ** 0.5, spread(stat[:, 4, :], D),
                                         ALU.mult, ALU.mult).then_inc(s_xn, 1)

            def embed(b):
                dve.wait_ge(s_emb[b], 16 * SLOTS)
                dve.wait_ge(s_halo[b], 16)
                dve.wait_ge(s_halo0[b], 16)
                rows = emb[:, b, :, :].rearrange("p k c -> p (k c)")
                shifted = bass.AP(tensor=rows.tensor, offset=rows.offset,
                                  ap=[rows.ap[0], [C * D, SLOTS], [1, D], [C * D + D, C]])
                link(dve.reduce_sum(h[:, b, :, :], shifted, AX.X))
                return norm_sums(h[:, b, :, :])

            def key_sums(b):
                dve.wait_ge(s_kv, b + 1)
                kv = QP0[:, :].rearrange("p (t c) -> p t c", c=2 * D)
                if b >= 2:
                    dve.wait_ge(s_pv, (b - 1) * PAIRS)
                dve.tensor_copy(v[b % 2][:, :, :], kv[:, :, D:2 * D]).then_inc(s_kv_read, 1)
                ins = dve.tensor_copy(kq[:, 0], kv[:, :, 0:D])
                ins.then_inc(s_kv_read, 1)
                dve.wait_ge(s_kv_read, 2 * b + 2)
                link(dve.tensor_tensor(kq[:, 1], kq[:, 0], kq[:, 0], ALU.mult))
                link(dve.reduce_sum(kstat[:, 0, :], kq[:, 1], AX.X))
                return ask_root(dve.tensor_scalar(kstat[:, 1, :], kstat[:, 0, :], D * RMS_EPS, None, ALU.add))

            def key_stack(asked, b):
                refine(asked, kstat)
                if b:
                    dve.wait_ge(s_kp, b)
                link(dve.scalar_tensor_tensor(kq[:, 1], kq[:, 0], -0.5, spread(kstat[:, 4, :], D),
                                              ALU.mult, ALU.mult))
                cos = ec("k_cos").rearrange("p (t d) -> p t d", d=D)
                sin = ec("k_sin").rearrange("p (t d) -> p t d", d=D)
                dve.tensor_tensor(kq[:, 0], kq[:, 1], cos, ALU.mult).then_inc(s_krot, 1)
                for e in range(2):
                    dve.tensor_tensor(kq[:, 2, :, e::2], kq[:, 1, :, 1 - e::2], sin[:, :, e::2],
                                      ALU.mult).then_inc(s_krot, 1)
                dve.wait_ge(s_krot, 3 * b + 3)
                link(dve.tensor_tensor(kq[:, 3], kq[:, 0], kq[:, 2], ALU.add))
                link(dve.tensor_tensor(ktok[:, :, 0, :], kq[:, 3], gs[:, :].unsqueeze(1).broadcast_to([P, TILES, D]),
                                       ALU.mult))
                sign = ec("swap_sign")
                for e in range(2):
                    dve.tensor_tensor(ktok[:, :, 1, e::2], ktok[:, :, 0, 1 - e::2],
                                      sign[:, e::2].unsqueeze(1).broadcast_to([P, TILES, D // 2]),
                                      ALU.mult).then_inc(s_ktok, 1)

            def query_sums(b, t):
                n = b * TILES + t
                q = qstat[t % 2]
                dve.wait_ge(s_qsq, 2 * n + 2)
                ins = dve.reduce_sum(q[:, 0, :], qsq[t % 2][:, :, :], AX.X)
                ins.then_inc(s_qsum, 1)
                dve.wait_ge(s_qsum, n + 1)
                return ask_root(dve.tensor_scalar(q[:, 1, :], q[:, 0, :], D * RMS_EPS, None, ALU.add))

            def query_scale(asked, b, t):
                refine(asked, qstat[t % 2])
                if b >= 2:
                    dve.wait_ge(s_qt, (b - 1) * H)
                for i, bk in enumerate(q_banks(b, t)):
                    ins = dve.scalar_tensor_tensor(qs[b % 2][:, t, 8 * i:8 * i + 8, 0, :],
                                                   bk[:, :].rearrange("p (h d) -> p h d", d=D), -0.5,
                                                   spread(qstat[t % 2][:, 4, 8 * i:8 * i + 8], D), ALU.mult, ALU.mult)
                ins.then_inc(s_qs, 1)

            asked = {}

            def middle(b, slot):
                if slot == 7 and b + 1 < B:
                    asked["x"] = embed(b + 1)
                if b < B:
                    if slot == 0:
                        norm_scale(asked["x"], b)
                    elif slot == 1:
                        asked["k"] = key_sums(b)
                    elif slot == 2:
                        key_stack(asked["k"], b)
                    elif 3 <= slot <= 6:
                        query_scale(query_sums(b, slot - 3), b, slot - 3)

            def rotate(n):
                dve.wait_ge(s_qt, n + 1)
                if n >= 4:
                    dve.wait_ge(s_sc, 2 * (n - 3))
                dve.tensor_tensor(qst[n % 4][:, :], QT[:, :], ec("trig"), ALU.mult).then_inc(s_qst, 1)

            def divide(n):
                dve.wait_ge(s_r0, n + 1)
                link(dve.tensor_tensor(nw[:, 0], DN[:, :], r0[:, :], ALU.mult))
                link(dve.scalar_tensor_tensor(nw[:, 1], nw[:, 0], 2.0, r0[:, :], ALU.subtract, ALU.mult))
                b = n // PAIRS
                if b:
                    dve.wait_ge(s_yTp, b)
                dve.scalar_tensor_tensor(oT[:, n % PAIRS, :], OP[:, :], -1.0, nw[:, 1],
                                         ALU.mult, ALU.mult).then_inc(s_oT, 1)

            def add_y(b):
                dve.wait_ge(s_y, b + 1)
                dve.tensor_tensor(h[:, b, :, :], h[:, b, :, :], QP1[:, 0:SLOTS * D].rearrange("p (j d) -> p j d", d=D),
                                  ALU.add).then_inc(s_h, 1)

            dve.wait_ge(s_early, 16)
            link(dve.tensor_tensor(gs[:, :], ec("qn"), ec("kn"), ALU.mult))
            link(dve.tensor_scalar(gs[:, :], gs[:, :], float(D) ** 0.5, None, ALU.mult))
            link(dve.tensor_scalar(sq[:, 1, :], gs[:, :], -1.0, None, ALU.mult))
            link(dve.tensor_tensor(sq[:, 0, :], gs[:, :], sq[:, 1, :], ALU.max))
            link(dve.reduce_max(shift[:, 0:1], sq[:, 0, :], AX.X))
            link(dve.tensor_scalar(shift[:, 1:2], shift[:, 0:1], -1.0, 80.0, ALU.mult, ALU.add))
            dve.tensor_scalar(shift[:, 1:2], shift[:, 1:2], 0.0, None, ALU.min).then_inc(s_shift, 1)
            norm_scale(embed(0), 0)
            key_root = key_sums(0)
            asked["x"] = embed(1)
            sums = {0: query_sums(0, 0)}
            key_stack(key_root, 0)
            for t in range(TILES):
                if t + 1 < TILES:
                    sums[t + 1] = query_sums(0, t + 1)
                query_scale(sums[t], 0, t)
            rotate(0)
            rotate(1)
            for b in range(B):
                for p in range(PAIRS):
                    n = b * PAIRS + p
                    last_of_all = n == B * PAIRS - 1
                    if not last_of_all:
                        rotate(2 * n + 2)
                    if p == 2 and b:
                        add_y(b - 1)
                    middle(b + 1, p)
                    if not last_of_all:
                        rotate(2 * n + 3)
                    if n:
                        divide(n - 1)
            divide(B * PAIRS - 1)
            add_y(B - 1)

            dve.wait_ge(s_late, 16)
            before = lc("before").rearrange("p (e f) -> p e f", f=E)

            def last_layers(b):
                for i in range(2):
                    dve.wait_ge(s_f3, 3 * b + 2 + i)
                    ins = dve.tensor_tensor(
                        eo2[:, :, 2 * i:2 * i + 2, :], L3[i][:, :].rearrange("p (j e d) -> p j e d", e=2, d=D),
                        gw[b % 2][:, :, 2 * i:2 * i + 2].unsqueeze(3).broadcast_to([P, SLOTS, 2, D]), ALU.mult)
                    ins.then_inc(s_l3, 1)
                dve.wait_ge(s_base, 6 * b + 6)
                dve.tensor_tensor(fsum[:, 1], L3[2][:, 0:SLOTS * D].rearrange("p (j d) -> p j d", d=D), base[:, 4],
                                  ALU.add).then_inc(s_l3, 1)
                dve.wait_ge(s_l3, 3 * b + 3)
                link(dve.reduce_sum(fsum[:, 0], eo2[:, :, :, :].rearrange("p j e d -> p j d e"), AX.X))
                dve.tensor_tensor(h[:, b, :, :], fsum[:, 0], fsum[:, 1], ALU.add).then_inc(s_fin, 1)

            norm_scale(norm_sums(h[:, 0, :, :]), B)
            for b in range(B):
                dve.wait_ge(s_g, b + 1)
                logits = bank[0][:, 0:SLOTS * E].rearrange("p (j e) -> p j e", e=E)
                ins = dve.tensor_copy(ge[:, 7], logits)
                ins.then_inc(s_gc, 1)
                dve.wait_ge(s_gc, b + 1)
                link(dve.reduce_max(gst[:, 0, :], ge[:, 7], AX.X))
                dve.tensor_tensor(ge[:, 0], ge[:, 7], spread(gst[:, 0, :], E), ALU.subtract).then_inc(s_gx, 1)
                if b + 1 < B:
                    next_norm = norm_sums(h[:, b + 1, :, :])
                dve.wait_ge(s_ge, b + 1)
                link(dve.reduce_sum(gst[:, 1, :], ge[:, 1], AX.X))
                link(dve.reciprocal(gst[:, 4, :], gst[:, 1, :]))
                link(dve.tensor_tensor(ge[:, 2], ge[:, 1], spread(gst[:, 4, :], E), ALU.mult))
                link(dve.reduce_max(gst[:, 2, :], ge[:, 2], AX.X))
                dve.tensor_tensor(ge[:, 3], ge[:, 2], spread(gst[:, 2, :], E), ALU.subtract).then_inc(s_gp, 1)
                if b + 1 < B:
                    norm_scale(next_norm, B + b + 1)
                mine = ge[:, 2].unsqueeze(3).broadcast_to([P, SLOTS, E, E])
                other = ge[:, 2].unsqueeze(2).broadcast_to([P, SLOTS, E, E])
                link(dve.tensor_tensor(gcmp[:, 0], other, mine, ALU.is_gt))
                link(dve.tensor_tensor(gcmp[:, 1], other, mine, ALU.is_equal))
                link(dve.tensor_tensor(gcmp[:, 2], gcmp[:, 1], before.unsqueeze(1).broadcast_to([P, SLOTS, E, E]),
                                       ALU.mult))
                link(dve.tensor_tensor(gcmp[:, 1], gcmp[:, 0], gcmp[:, 2], ALU.add))
                link(dve.reduce_sum(ge[:, 5], gcmp[:, 1], AX.X))
                link(dve.tensor_scalar(ge[:, 6], ge[:, 5], 1.5, None, ALU.is_lt))
                dve.wait_ge(s_gw, b + 1)
                link(dve.tensor_tensor(ge[:, 5], ge[:, 4], ge[:, 6], ALU.mult))
                link(dve.reduce_sum(gst[:, 3, :], ge[:, 5], AX.X))
                link(dve.reciprocal(gst[:, 5, :], gst[:, 3, :]))
                if b >= 2:
                    dve.wait_ge(s_base, 6 * (b - 1))
                dve.tensor_tensor(gw[b % 2][:, :, :], ge[:, 5], spread(gst[:, 5, :], E), ALU.mult).then_inc(s_gwt, 1)
                dve.wait_ge(s_gwt, b + 1)
                if b:
                    last_layers(b - 1)
            last_layers(B - 1)

        @block.tensor
        def _(pe):
            def transpose_x(n):
                pe.wait_ge(s_xn, n + 1)
                if n == 0:
                    pe.wait_ge(s_early, 16)
                elif n < B:
                    pe.wait_ge(s_kst, n)
                elif n == B:
                    pe.wait_ge(s_kst, B)
                else:
                    pe.wait_ge(s_gc, n - B)
                for j in range(SLOTS):
                    last = pe.transpose(QP0[0:D, j * P:(j + 1) * P], xn[:, j, :], ident)
                last.then_inc(s_xTp, 1)

            def project_kv(b):
                pe.wait_ge(s_xT, b + 1)
                pe.wait_ge(s_w64, 32)
                for t in range(TILES):
                    last = pe.matmul(QP0[:, t * 2 * D:(t + 1) * 2 * D], xT[0:D, t * P:(t + 1) * P], wc("wkv"),
                                     start=True, stop=True)
                last.then_inc(s_kv, 1)

            def project_q(b, t):
                if t == 0:
                    pe.wait_ge(s_kv_read, 2 * b + 2)
                    if b >= 2:
                        pe.wait_ge(s_h, b - 1)
                elif b:
                    pe.wait_ge(s_qs, b * TILES + t)
                for i, bk in enumerate(q_banks(b, t)):
                    last = pe.matmul(bk[:, :], xT[0:D, t * P:(t + 1) * P], wc("wq")[:, 512 * i:512 * i + 512],
                                     start=True, stop=True)
                last.then_inc(s_q, 1)

            def transpose_k(b):
                pe.wait_ge(s_ktok, 2 * b + 2)
                pe.wait_ge(s_qs, (b + 1) * TILES)
                for t in range(TILES):
                    last = pe.transpose(QP0[:, t * P:(t + 1) * P], ktok[:, t].rearrange("p a d -> p (a d)"), ident)
                last.then_inc(s_kp, 1)

            def end(b, slot):
                if b < B:
                    if slot == 0:
                        transpose_x(b)
                    elif 2 <= slot <= 5:
                        project_q(b, slot - 2)
                    elif slot == 6:
                        transpose_k(b)

            def transpose_q(n):
                b, head = n // H, n % H
                if head == 0:
                    pe.wait_ge(s_qd, (b + 1) * TILES)
                if n:
                    pe.wait_ge(s_qst, n)
                for t in range(TILES):
                    src = qs[b % 2][:, t, head].rearrange("p a d -> p (a d)")
                    last = pe.transpose(QT[:, t * P:(t + 1) * P], src, ident)
                last.then_inc(s_qt, 1)

            def scores(n):
                if n % H == 0:
                    pe.wait_ge(s_kst, n // H + 1)
                pe.wait_ge(s_qst, n + 1)
                for half in range(2):
                    u = 2 * n + half
                    if u >= 3:
                        pe.wait_ge(s_p, u - 2)
                    bk = SC[u % 3]
                    for kt, c, w in HALVES[half]:
                        for odd in range(2):
                            o = D * odd
                            seen = slice(o, min(o + P + D, w))
                            last = pe.matmul(bk[o:o + D, c + seen.start:c + seen.stop],
                                             kst[n // H % 2][:, kt * P + o:kt * P + o + D],
                                             qst[n % 4][:, kt * P + seen.start:kt * P + seen.stop],
                                             start=True, stop=True, skip_group_check=True)
                    last.then_inc(s_sc, 1)

            def weigh(n):
                if n % PAIRS == 0:
                    pe.wait_ge(s_kv_read, 2 * (n // PAIRS) + 1)
                pe.wait_ge(s_m, 4 * n + 4)
                if n:
                    pe.wait_ge(s_oT, n)
                for t in range(TILES):
                    w = WIN if t < TILES - 1 else P
                    for hh in range(2):
                        pe.matmul(OP[D * hh:D * hh + D, t * P:t * P + w], v[n // PAIRS % 2][:, t, :],
                                  pT[n % 2][:, hh, t * WIN:t * WIN + w],
                                  start=(t == 0), stop=(t == TILES - 1), skip_group_check=True)
                for hh in range(2):
                    pe.matmul(DN[D * hh:D * hh + D, 0:P], ones[:, :], pT[n % 2][:, hh, 0:P], start=True, stop=False,
                              skip_group_check=True)
                pe.wait_ge(s_ps, 2 * n + 2)
                for hh in range(2):
                    last = pe.matmul(DN[D * hh:D * hh + D, P:S], ones[:, :],
                                     pS[n % 2][:, hh].rearrange("p t w -> p (t w)"), start=False, stop=True,
                                     skip_group_check=True)
                last.then_inc(s_pv, 1)

            def output_T(b):
                if b == 0:
                    pe.wait_ge(s_late, 16)
                pe.wait_ge(s_oT, (b + 1) * PAIRS)
                for q in range(PAIRS // 2):
                    for odd in range(2):
                        p = 2 * q + odd
                        last = pe.matmul(QP1[D * odd:D * odd + D, :], lc("wo")[:, p * D:(p + 1) * D], oT[:, p, :],
                                         start=(q == 0), stop=(q == PAIRS // 2 - 1), skip_group_check=True)
                last.then_inc(s_yTp, 1)

            def output(b):
                pe.wait_ge(s_yT, b + 1)
                yv = yT[:, :].rearrange("d (p j) -> d j p", j=SLOTS)
                for j in range(SLOTS):
                    last = pe.matmul(QP1[:, j * D:(j + 1) * D], yv[:, j, :], ec("ident2"), start=True, stop=True)
                last.then_inc(s_y, 1)

            transpose_x(0)
            project_kv(0)
            for t in range(TILES):
                project_q(0, t)
            transpose_k(0)
            transpose_q(0)
            transpose_q(1)
            pe.wait_ge(s_ones, 2)
            for b in range(B):
                for p in range(PAIRS):
                    n = b * PAIRS + p
                    scores(2 * n)
                    if n + 1 < B * PAIRS:
                        transpose_q(2 * n + 2)
                    if p == 1 and b + 1 < B:
                        project_kv(b + 1)
                    if p == 1 and b:
                        output_T(b - 1)
                    scores(2 * n + 1)
                    if n + 1 < B * PAIRS:
                        transpose_q(2 * n + 3)
                    if n:
                        weigh(n - 1)
                    end(b + 1, p)
                    if p == 1 and b:
                        output(b - 1)
            weigh(B * PAIRS - 1)
            output_T(B - 1)
            output(B - 1)

            def gates(b):
                pe.wait_ge(s_xT, B + b + 1)
                for j in range(SLOTS):
                    last = pe.matmul(bank[0][:, j * E:(j + 1) * E], xT[:, j * P:(j + 1) * P], wc("gW", D + 1),
                                     start=True, stop=True)
                last.then_inc(s_g, 1)

            def first(b, i):
                n = (E + 1) * b + i
                if n == 0:
                    pe.wait_ge(s_h, B)
                elif n >= 3:
                    pe.wait_ge(s_f1r, n - 2)
                if i == 0:
                    pe.matmul(L1[n % 3][0:SH1, :], wc("sW1"), xT[0:D, :], start=True, stop=True).then_inc(s_f1, 1)
                else:
                    pe.matmul(L1[n % 3][:, :], wc("eW1")[:, (i - 1) * EH1:i * EH1], xT[0:D, :],
                              start=True, stop=True).then_inc(s_f1, 1)

            def second(b, i):
                pe.wait_ge(s_f1r, (E + 1) * b + (1, 3, 5)[i])
                if 3 * b + i:
                    pe.wait_ge(s_f2r, 3 * b + i)
                if i == 0:
                    last = pe.matmul(L2[:, :], wc("sW2", SH1), hs1[:, :], start=True, stop=True)
                for k in range(2 if i else 0):
                    e = 2 * (i - 1) + k
                    last = pe.matmul(L2[D * k:D * k + D, :], lc("eW2")[:, e * EH2:(e + 1) * EH2],
                                     he1[:, e, :], start=True, stop=True)
                last.then_inc(s_f2, 1)

            def third(b, i):
                pe.wait_ge(s_f2r, 3 * b + i + 1)
                if b:
                    pe.wait_ge(s_fin, b)
                for j in range(SLOTS):
                    if i == 0:
                        last = pe.matmul(L3[2][:, j * D:(j + 1) * D], hs2[:, j * P:(j + 1) * P], lc("sW3"),
                                         start=True, stop=True)
                    else:
                        last = pe.matmul(L3[i - 1][:, j * P:(j + 1) * P], he2[:, i - 1, j * P:(j + 1) * P],
                                         lc("eW3")[:, (i - 1) * P:i * P], start=True, stop=True)
                last.then_inc(s_f3, 1)

            transpose_x(B)
            gates(0)
            for b in range(B):
                first(b, 0)
                first(b, 1)
                if b:
                    third(b - 1, 2)
                first(b, 2)
                second(b, 0)
                first(b, 3)
                second(b, 1)
                first(b, 4)
                if b + 1 < B:
                    transpose_x(B + b + 1)
                third(b, 0)
                third(b, 1)
                second(b, 2)
                if b + 1 < B:
                    gates(b + 1)
            third(B - 1, 2)


def _tables():
    f32 = np.float32
    freqs = np.power(f32(10000.0), (f32(-2.0) * np.arange(D // 2, dtype=f32) / f32(D)).astype(f32)).astype(f32)
    theta = (np.arange(S, dtype=f32)[:, None] * freqs[None, :]).astype(f32)
    cos, sin = np.repeat(np.cos(theta), 2, 1), np.repeat(np.sin(theta), 2, 1)
    sign = np.tile(np.array([-1.0, 1.0], f32), D // 2)
    by_tile = lambda a: a.reshape(TILES, P, D).transpose(1, 0, 2).reshape(P, TILES * D)
    e = np.arange(E)
    return {
        "ident": np.eye(P, dtype=f32), "trig": np.concatenate([cos.T, sin.T], 0),
        "k_cos": by_tile(cos), "k_sin": by_tile(sin * sign),
        "swap_sign": np.tile(-sign, (P, 1)), "ident2": np.tile(np.eye(D, dtype=f32), (2, 1)),
        "before": np.tile((e[None, :] < e[:, None]).astype(f32).reshape(1, E * E), (P, 1)),
    }


def _pack(where, width, rows, parts):
    a = np.zeros((rows, width), np.float32)
    for name, part in parts.items():
        o, w = where[name]
        assert part.shape[1] == w, name
        a[:part.shape[0], o:o + w] = part
    return a


def kernel(**inputs):
    import concourse.bacc as bacc
    from concourse.bass_utils import run_bass_kernel_spmd

    i = {k.replace("L0_", ""): np.asarray(a) for k, a in inputs.items()}
    t = _tables()
    rows = lambda a: np.tile(a.reshape(1, -1), (P, 1))
    early = _pack(EARLY, EARLY_W, P, {**{k: t[k] for k in ("ident", "trig", "k_cos", "k_sin", "swap_sign", "ident2")},
                                      "qn": rows(i["attn_q_norm_w"]), "kn": rows(i["attn_k_norm_w"])})
    eW3 = np.zeros((P, 2, 2, D), np.float32)
    for e in range(E):
        eW3[D * (e % 2):D * (e % 2) + D, e // 2, e % 2] = i["ffn_eW3"][e]
    late = _pack(LATE, LATE_W, P, {
        "wo": i["attn_wo"].T.reshape(PAIRS, P, D).transpose(1, 0, 2).reshape(P, -1),
        "eW2": i["ffn_eW2"].transpose(1, 0, 2).reshape(EH1, -1), "sW3": i["ffn_sW3"], "eW3": eW3.reshape(P, -1),
        "eb1": i["ffn_eb1"].T, "eb2": i["ffn_eb2"].reshape(2, P).T, "sb2": i["ffn_sb2"].reshape(-1, 1),
        "sb1": i["ffn_sb1"].reshape(-1, 1), "eb3": rows(i["ffn_eb3"]), "sb3": rows(i["ffn_sb3"]),
        "before": t["before"]})
    w64 = _pack(W64, W64_W, D, {
        "wq": i["attn_wq"].T, "wkv": i["attn_wkv"].T, "sW1": i["ffn_sW1"],
        "eW1": i["ffn_eW1"].transpose(1, 0, 2).reshape(D, -1), "sW2": i["ffn_sW2"], "gW": i["ffn_gW"]})
    arrays = {
        "tok": np.ascontiguousarray(i["x"].reshape(B, P, SLOTS).transpose(1, 0, 2).reshape(P, B * SLOTS)),
        "table": np.ascontiguousarray(i["tok_emb_table"].reshape(-1, C * D)),
        "early": early, "late": late, "w64": w64,
        "gb": np.ascontiguousarray(i["ffn_gb"].reshape(1, E)),
    }
    nc = bacc.Bacc("TRN2", target_bir_lowering=False, num_devices=1)
    aps = [nc.dram_tensor("in_" + n, a.shape, mybir.dt.from_np(a.dtype), kind="ExternalInput").ap()
           for n, a in arrays.items()]
    out = nc.dram_tensor("out_h", (B, S, D), FP32, kind="ExternalOutput").ap()
    build(nc, *aps, out)
    r = run_bass_kernel_spmd(nc, [{"in_" + n: a for n, a in arrays.items()}], core_ids=[0])
    return r.results[0]["out_h"]
```

```python
import concourse.bass as bass
import concourse.mybir as mybir
import numpy as np
from contextlib import ExitStack

FP32 = mybir.dt.float32
I32 = mybir.dt.int32
ALU = mybir.AluOpType
ACT = mybir.ActivationFunctionType
AX = mybir.AxisListType

B, S, D = 4, 512, 64
C = 5
H = 16
PAIRS = H // 2
P = 128
TILES = S // P
SLOTS = S // P
WIN = 2 * P
E, EH1, EH2, SH1, SH2 = 4, 128, 64, 64, 128
LN_EPS, RMS_EPS = 1e-5, 1.1920929e-07

def _columns(parts):
    at, where = 0, {}
    for name, width in parts:
        where[name] = (at, width)
        at += width
    return where, at

EARLY, EARLY_W = _columns([("ident", P), ("cos", TILES * D), ("sin", TILES * D), ("qn", D), ("kn", D), ("ident2", D)])
LATE, LATE_W = _columns([("wo", PAIRS * D), ("eW2", E * EH2), ("sW3", D), ("eW3", 2 * P), ("eb1", E),
                         ("eb2", 2), ("sb2", 1), ("sb1", 1), ("eb3", E * D), ("sb3", D), ("before", E * E)])
W64, W64_W = _columns([("wq", H * D), ("wkv", 2 * D), ("sW1", SH1), ("eW1", E * EH1), ("sW2", SH2), ("gW", E)])

NORM = {what: i for i, what in enumerate([("x", 0), ("x", 1), ("x", 2), ("f", 0), ("x", 3), ("f", 1), ("f", 2),
                                          ("f", 3)])}


def build(nc, tok, table, early_d, late_d, w64_d, gb_d, out):
    with ExitStack() as ctx:
        def sb(name, shape, dt=FP32):
            return ctx.enter_context(nc.sbuf_tensor(name, shape, dt))

        def sem(name):
            return ctx.enter_context(nc.semaphore(name))

        idx = sb("idx", [P, B * SLOTS], I32)
        emb = sb("emb", [P, B, 2 * SLOTS, C * D])
        early = sb("early", [P, EARLY_W])
        late = sb("late", [P, LATE_W])
        w64 = sb("w64", [D + 1, W64_W])
        ones = sb("ones", [P, D])
        gs = sb("gs", [P, D])
        shift = sb("shift", [P, 2])
        h = sb("h", [P, B, SLOTS, D])
        xc = sb("xc", [P, SLOTS, D])
        sq = sb("sq", [P, SLOTS, D])
        xn = sb("xn", [P, SLOTS, D])
        stat = sb("stat", [P, 8, SLOTS])
        xT = sb("xT", [D, S])
        fxT = sb("fxT", [D + 1, S])
        kq = sb("kq", [P, 4, TILES, D])
        kstat = sb("kstat", [P, 5, TILES])
        ktok = sb("ktok", [P, TILES, 2, D])
        kst = [sb(f"kst{i}", [P, 2, S]) for i in range(2)]
        v = [sb(f"v{i}", [P, TILES, D]) for i in range(2)]
        qsq = [sb(f"qsq{i}", [P, H, D]) for i in range(2)]
        qstat = [sb(f"qstat{i}", [P, 5, H]) for i in range(2)]
        qn = sb("qn", [P, TILES, H, D])
        qcos = sb("qcos", [P, H * D])
        qsin = sb("qsin", [P, H * D])
        qs = sb("qs", [P, TILES, H, D])
        qst = [sb(f"qst{i}", [P, S]) for i in range(2)]
        pT = [sb(f"pT{i}", [P, 2, 4 * WIN - P]) for i in range(2)]
        pS = [sb(f"pS{i}", [P, 2, TILES - 1, P]) for i in range(2)]
        oT = sb("oT", [P, PAIRS, S])
        r0 = sb("r0", [P, S])
        nw = sb("nw", [P, S])
        def reuse(b, at, width):
            return emb[:, b, :, :].rearrange("p k c -> p (k c)")[:, at:at + width]

        yT = reuse(0, 0, S)
        hs1 = reuse(0, 0, S)[0:SH1, :]
        hs2 = reuse(0, S, S)
        he2 = reuse(0, 2 * S, 2 * S).rearrange("p (i s) -> p i s", s=S)
        gcmp = reuse(0, 4 * S, 3 * SLOTS * E * E).rearrange("p (i j e f) -> p i j e f", i=3, j=SLOTS, e=E)
        wb = reuse(1, 0, SLOTS * E * D).rearrange("p (j e d) -> p j e d", e=E, d=D)
        base = reuse(1, SLOTS * E * D, 5 * SLOTS * D).rearrange("p (i j d) -> p i j d", i=5, d=D)
        he1 = reuse(2, 0, E * S).rearrange("p (e s) -> p e s", s=S)
        fsum = reuse(2, E * S, 2 * SLOTS * D).rearrange("p (i j d) -> p i j d", i=2, d=D)
        eo2 = sb("eo2", [P, SLOTS, E, D])
        ge = sb("ge", [P, 8, SLOTS, E])
        gw = [sb(f"gw{i}", [P, SLOTS, E]) for i in range(2)]
        gst = sb("gst", [P, 6, SLOTS])
        bank = [ctx.enter_context(nc.psum_tensor(f"bank{i}", [P, 512], FP32)) for i in range(8)]
        QP0, QP1, QT, OP, DN = bank[0], bank[1], bank[2], bank[6], bank[7]
        SC = bank[3:5]

        def ffn_bank(f, stage):
            if f == B - 1:
                return bank[{"T": 0, "G": 2, "F0": 3, "F1": 4, "F2": 5, "F3": 6, "F4": 7,
                             "S0": 0, "S1": 2, "S2": 3, "L1": 4, "L2": 5, "L0": 6}[stage]]
            return {"F3": QP1, "S0": QP0, "S2": QP1, "L2": QP1}.get(stage, bank[5])
        def y_banks(b):
            return (QT, QP0) if b == B - 1 else (QP1, QP1)

        def k_bank(b):
            return bank[3] if b == 0 else QP0

        def unit(b, t, half):
            return TILES * half + t if b == 0 else 2 * TILES * b + 2 * t + half

        def q_bank(b, t, half):
            if b == 0:
                return bank[([3, 4, 5, 6] if half == 0 else [0, 1, 7, 5])[t]]
            return (QP0, QP1)[half]

        def ec(name):
            o, w = EARLY[name]
            return early[:, o:o + w]

        def lc(name, rows=P):
            o, w = LATE[name]
            return late[0:rows, o:o + w]

        def wc(name, rows=D):
            o, w = W64[name]
            return w64[0:rows, o:o + w]

        ident = ec("ident")

        s_idx = sem("s_idx")
        s_halo0 = [sem(f"s_halo0_{b}") for b in range(B)]
        s_h0 = sem("s_h0")
        s_emb = [sem(f"s_emb{b}") for b in range(B)]
        s_halo = [sem(f"s_halo{b}") for b in range(B)]
        s_early = sem("s_early")
        s_late = sem("s_late")
        s_w64 = sem("s_w64")
        s_ones = sem("s_ones")
        s_warm = sem("s_warm")
        s_shift = sem("s_shift")
        s_xn = sem("s_xn")
        s_xTp = sem("s_xTp")
        s_xT = sem("s_xT")
        s_fxT = sem("s_fxT")
        s_kv = sem("s_kv")
        s_kv_read = sem("s_kv_read")
        s_kn = sem("s_kn")
        s_krot = sem("s_krot")
        s_ktok = sem("s_ktok")
        s_kp = sem("s_kp")
        s_kst = sem("s_kst")
        s_q = sem("s_q")
        s_qsq = sem("s_qsq")
        s_qs = sem("s_qs")
        s_qr = sem("s_qr")
        s_qt = sem("s_qt")
        s_qst = sem("s_qst")
        s_sc = sem("s_sc")
        s_p = sem("s_p")
        s_pv = sem("s_pv")
        s_m = sem("s_m")
        s_ps = sem("s_ps")
        s_ln = sem("s_ln")
        s_r0 = sem("s_r0")
        s_qsum = sem("s_qsum")
        s_oT = sem("s_oT")
        s_yTp = sem("s_yTp")
        s_yT = sem("s_yT")
        s_y = sem("s_y")
        s_h = sem("s_h")
        s_f1 = sem("s_f1")
        s_f1r = sem("s_f1r")
        s_f2 = sem("s_f2")
        s_f2r = sem("s_f2r")
        s_g = sem("s_g")
        s_gc = sem("s_gc")
        s_gx = sem("s_gx")
        s_ge = sem("s_ge")
        s_gp = sem("s_gp")
        s_gw = sem("s_gw")
        s_gwt = sem("s_gwt")
        s_base = sem("s_base")
        s_f3 = sem("s_f3")
        s_l3 = sem("s_l3")
        s_fin = sem("s_fin")
        s_out = sem("s_out")
        s_dve = sem("s_dve")
        s_sum = sem("s_sum")
        s_log = sem("s_log")
        s_root = sem("s_root")

        block = ctx.enter_context(nc.Block())

        HALVES = [[(0, 0, WIN), (1, WIN, WIN)], [(2, 0, WIN), (3, WIN, P)]]
        HALF_W = [2 * WIN, WIN + P]

        @block.sync
        def _(sp):
            sp.dma_start(idx[:, :], tok).then_inc(s_idx, 16)
            for b in range(B):
                sp.dma_start(emb[P - 1:P, b, SLOTS:, :],
                             table[0:1, :].unsqueeze(1).broadcast_to([1, SLOTS, C * D])).then_inc(s_halo0[b], 16)
                sp.wait_ge(s_emb[b], 16 * SLOTS)
                sp.dma_start(emb[0:P - 1, b, SLOTS:, :], emb[1:P, b, 0:SLOTS, :]).then_inc(s_halo[b], 16)
                if b == 0:
                    sp.dma_start(w64[0:D, :], w64_d).then_inc(s_w64, 16)
                    sp.dma_start(w64[D:D + 1, W64["gW"][0]:W64["gW"][0] + E], gb_d).then_inc(s_w64, 16)
            sp.dma_start(late[:, :], late_d).then_inc(s_late, 16)
            for b in range(B):
                sp.wait_ge(s_fin, b + 1)
                sp.dma_start(out[b].rearrange("(p j) d -> p j d", j=SLOTS), h[:, b, :, :]).then_inc(s_out, 16)
            sp.wait_ge(s_out, 16 * B)

        @block.gpsimd
        def _(pool):
            pool.memset(ones[:, :], 1.0).then_inc(s_ones, 1)
            pool.wait_ge(s_ones, 1)
            pool.memset(fxT[D:D + 1, :], 1.0).then_inc(s_ones, 1)
            pool.wait_ge(s_ones, 2)
            pool.wait_ge(s_idx, 16)
            for b in range(B):
                for j in range(SLOTS):
                    pool.indirect_dma_start(
                        out=emb[:, b, j, :], out_offset=None, in_=table,
                        in_offset=bass.IndirectOffsetOnAxis(ap=idx[:, b * SLOTS + j:b * SLOTS + j + 1], axis=0),
                    ).then_inc(s_emb[b], 16)

            def strided(first, step, count):
                return bass.AP(tensor=first.tensor, offset=first.offset,
                               ap=[first.ap[0], [step, count], first.ap[-1]])

            def mask(n):
                own = pT[n % 2][:, :, 0:(TILES - 1) * WIN].rearrange("p h (t w) -> p h t w", w=WIN)
                for hh in range(2):
                    pool.wait_ge(s_p, 4 * n + 2 * hh + 2)
                    blocks = strided(pT[n % 2][:, hh, 0:P], WIN, TILES)
                    pool.affine_select(out=blocks, in_=blocks, compare_op=ALU.is_ge, fill=0.0, base=0,
                                       pattern=[[0, TILES], [1, P]], channel_multiplier=-1).then_inc(s_m, 1)
                    pool.wait_ge(s_m, 4 * n + 2 * hh + 1)
                    blocks = own[:, hh, :, P:WIN]
                    pool.affine_select(out=blocks, in_=blocks, compare_op=ALU.is_ge, fill=0.0, base=0,
                                       pattern=[[0, TILES - 1], [-1, P]], channel_multiplier=1).then_inc(s_m, 1)
                    pool.wait_ge(s_m, 4 * n + 2 * hh + 2)
                    if n >= 2:
                        pool.wait_ge(s_pv, n - 1)
                    nxt = strided(pT[n % 2][:, hh, WIN:WIN + P], WIN, TILES - 1)
                    pool.tensor_tensor(pS[n % 2][:, hh], nxt, own[:, hh, :, P:WIN], ALU.add).then_inc(s_ps, 1)
                    pool.wait_ge(s_ps, 2 * n + hh + 1)

            def base_steps(f, steps):
                weight = gw[f % 2][:, :, :].unsqueeze(3).broadcast_to([P, SLOTS, E, D])
                b3 = lc("eb3").rearrange("p (e d) -> p e d", d=D).unsqueeze(1).broadcast_to([P, SLOTS, E, D])
                sb3 = lc("sb3").unsqueeze(1).broadcast_to([P, SLOTS, D])
                for i in steps:
                    if i == 0:
                        pool.wait_ge(s_gwt, f + 1)
                        if f:
                            pool.wait_ge(s_fin, f)
                        pool.tensor_tensor(wb[:, :, :, :], weight, b3, ALU.mult).then_inc(s_base, 1)
                    else:
                        x, y = [(wb[:, :, 0, :], wb[:, :, 1, :]), (wb[:, :, 2, :], wb[:, :, 3, :]),
                                (base[:, 0], base[:, 1]), (base[:, 2], sb3), (base[:, 3], h[:, f, :, :])][i - 1]
                        pool.tensor_tensor(base[:, i - 1], x, y, ALU.add).then_inc(s_base, 1)
                    pool.wait_ge(s_base, 6 * f + i + 1)

            def key_stack(b):
                pool.wait_ge(s_kn, b + 1)
                if b:
                    pool.wait_ge(s_kp, b)
                steps = [4 * b]

                def step(ins):
                    steps[0] += 1
                    ins.then_inc(s_krot, 1)
                    pool.wait_ge(s_krot, steps[0])

                cos = ec("cos").rearrange("p (t d) -> p t d", d=D)
                sin = ec("sin").rearrange("p (t d) -> p t d", d=D)
                step(pool.tensor_tensor(kq[:, 0], kq[:, 1], cos, ALU.mult))
                for e in range(2):
                    step(pool.tensor_tensor(kq[:, 2, :, e::2], kq[:, 1, :, 1 - e::2], sin[:, :, e::2], ALU.mult))
                step(pool.tensor_tensor(kq[:, 3], kq[:, 0], kq[:, 2], ALU.add))
                for a in range(2):
                    pool.tensor_tensor(ktok[:, :, a, :], kq[:, 3], gs[:, :].unsqueeze(1).broadcast_to([P, TILES, D]),
                                       ALU.mult).then_inc(s_ktok, 1)
                    pool.wait_ge(s_ktok, 2 * b + a + 1)

            def embed(b):
                pool.wait_ge(s_emb[b], 16 * SLOTS)
                pool.wait_ge(s_halo[b], 16)
                pool.wait_ge(s_halo0[b], 16)
                part = lambda i: emb[:, b, i:i + SLOTS, i * D:(i + 1) * D]
                for i in range(1, C):
                    pool.tensor_tensor(h[:, b, :, :], part(0) if i == 1 else h[:, b, :, :], part(i),
                                       ALU.add).then_inc(s_h0, 1)
                    pool.wait_ge(s_h0, (b - 1) * (C - 1) + i)

            embed(1)
            key_stack(0)
            for b in range(B):
                for p in range(PAIRS):
                    mask(b * PAIRS + p)
                    if p == 2 and b + 1 < B:
                        key_stack(b + 1)
                    if p == 6 and b + 2 < B:
                        embed(b + 2)
                    if p == PAIRS - 1 and b:
                        base_steps(b - 1, range(0, 1))
                    elif p == 0 and b >= 2:
                        base_steps(b - 2, range(1, 6))
            base_steps(B - 2, range(1, 6))
            base_steps(B - 1, range(0, 6))

        @block.scalar
        def _(act):
            act.preload_act_table_set("natural_log_exp_and_others")
            act.dma_start(early[:, :], early_d).then_inc(s_early, 16)

            def keep_xT(b):
                act.wait_ge(s_xTp, NORM["x", b] + 1)
                src = QP0[0:D, :].rearrange("d (j p) -> d p j", j=SLOTS)
                act.activation(xT[:, :].rearrange("d (p j) -> d p j", j=SLOTS), src, ACT.Copy).then_inc(s_xT, 1)

            def keep_fxT(f):
                act.wait_ge(s_xTp, NORM["f", f] + 1)
                if f == 0:
                    act.wait_ge(s_ones, 2)
                    act.wait_ge(s_late, 16)
                else:
                    act.wait_ge(s_f1, (E + 1) * f)
                act.activation(fxT[0:D, :], ffn_bank(f, "T")[0:D, :], ACT.Copy).then_inc(s_fxT, 1)

            def relu_first(f, i):
                act.wait_ge(s_f1, (E + 1) * f + i + 1)
                if f:
                    act.wait_ge(s_f2, 3 * f)
                if i == 0:
                    act.wait_ge(s_y, f + 1)
                dst = hs1[:, :] if i == 0 else he1[:, i - 1, :]
                rows = SH1 if i == 0 else EH1
                act.activation(dst, ffn_bank(f, f"F{i}")[0:rows, :], ACT.Relu,
                               bias=lc("sb1", SH1) if i == 0 else lc("eb1")[:, i - 1:i]).then_inc(s_f1r, 1)

            def relu_second(f, i):
                act.wait_ge(s_f2, 3 * f + i + 1)
                if f:
                    act.wait_ge(s_f3, 3 * f)
                act.activation(hs2[:, :] if i == 0 else he2[:, i - 1, :], ffn_bank(f, f"S{i}")[:, :], ACT.Relu,
                               bias=lc("sb2") if i == 0 else lc("eb2")[:, i - 1:i]).then_inc(s_f2r, 1)

            def gate_exp(f):
                act.wait_ge(s_gx, f + 1)
                act.activation(ge[:, 1], ge[:, 0], ACT.Exp).then_inc(s_ge, 1)

            def weight_exp(f):
                act.wait_ge(s_gp, f + 1)
                act.activation(ge[:, 4], ge[:, 3], ACT.Exp).then_inc(s_gw, 1)

            def ffn_middle(f, slot):
                if f >= 0:
                    if slot == 6:
                        relu_first(f, 1)
                    elif slot == 7:
                        relu_first(f, 4)
                        relu_second(f, 0)

            def ffn_end(f, slot):
                if f >= 0:
                    if slot == 4:
                        keep_fxT(f)
                    elif slot == 5:
                        relu_first(f, 0)
                        gate_exp(f)
                    elif slot == 6:
                        weight_exp(f)
                        relu_first(f, 2)
                        relu_first(f, 3)
                    elif slot == 7:
                        relu_second(f, 1)
                        relu_second(f, 2)

            def square_q(b, t, halves=(0, 1)):
                for i in halves:
                    n = unit(b, t, i)
                    act.wait_ge(s_q, n + 1)
                    if b == 0 and t >= 2:
                        act.wait_ge(s_qsum, n - 1)
                    elif b:
                        act.wait_ge(s_qsum, 2 * TILES * b if t < 2 else unit(b, t - 1, 0))
                    act.activation(qsq[t % 2][:, 8 * i:8 * i + 8, :],
                                   q_bank(b, t, i)[:, :].rearrange("p (h d) -> p h d", d=D),
                                   ACT.Square).then_inc(s_qsq, 1)

            def keep_qst(n):
                act.wait_ge(s_qt, n + 1)
                if n >= 2:
                    act.wait_ge(s_sc, 4 * (n - 1))
                act.activation(qst[n % 2][:, :], QT[:, :], ACT.Copy).then_inc(s_qst, 1)

            def keep_kst(b):
                act.wait_ge(s_kp, b + 1)
                for a in range(2):
                    rows = slice(D * a, D * a + D)
                    act.activation(kst[b % 2][rows, a, :], k_bank(b)[rows, :], ACT.Copy).then_inc(s_kst, 1)

            roots = [0]

            def root(st):
                roots[0] += 1
                act.wait_ge(s_sum, roots[0])
                act.activation(st[:, 3, :], st[:, 1, :], ACT.Ln).then_inc(s_log, 1)
                act.wait_ge(s_log, roots[0])
                act.activation(st[:, 2, :], st[:, 3, :], ACT.Exp, scale=-0.5).then_inc(s_root, 1)

            def end(b, slot):
                if b < B:
                    if slot == 0:
                        keep_xT(b)
                    elif slot == 6:
                        keep_kst(b)
                    if 2 <= slot <= 5:
                        square_q(b, slot - 2)

            def near_reciprocal(n):
                act.wait_ge(s_pv, n + 1)
                if n:
                    act.wait_ge(s_oT, n)
                act.activation(r0[:, :], DN[:, :], ACT.Ln).then_inc(s_ln, 1)
                act.wait_ge(s_ln, n + 1)
                act.activation(r0[:, :], r0[:, :], ACT.Exp, scale=-1.0).then_inc(s_r0, 1)

            def keep_yT(b):
                act.wait_ge(s_yTp, b + 1)
                if b > 1:
                    act.wait_ge(s_f2, 3 * (b - 2) + 1)
                act.activation(yT[:, :], y_banks(b)[0][:, :], ACT.Copy).then_inc(s_yT, 1)

            root(stat)
            keep_xT(0)
            root(kstat)
            square_q(0, 0, (0,))
            for t in range(TILES):
                if t + 1 < TILES:
                    square_q(0, t + 1, (0,))
                root(qstat[t % 2][:, :, 0:8])
            keep_kst(0)
            square_q(0, 0, (1,))
            square_q(0, 1, (1,))
            keep_qst(0)
            root(stat)
            root(qstat[0][:, :, 8:16])
            root(qstat[1][:, :, 8:16])
            act.wait_ge(s_shift, 1)

            def exps(n, hh):
                for half in range(2):
                    u = 4 * n + 2 * hh + half
                    act.wait_ge(s_sc, u + 1)
                    w = HALF_W[half]
                    act.activation(pT[n % 2][:, hh, 2 * WIN * half:2 * WIN * half + w],
                                   SC[u % 2][:, 0:w], ACT.Exp, bias=shift[:, 1:2]).then_inc(s_p, 1)

            for b in range(B):
                for p in range(PAIRS):
                    n = b * PAIRS + p
                    if n >= 2:
                        act.wait_ge(s_pv, n - 1)
                    exps(n, 0)
                    if n + 1 < B * PAIRS and p < PAIRS - 1:
                        keep_qst(n + 1)
                    if n == 0:
                        square_q(0, 2, (1,))
                        square_q(0, 3, (1,))
                    if p == 1 and b:
                        keep_yT(b - 1)
                    ffn_middle(b - 1, p)
                    if 3 <= p <= 6 and b + 1 < B:
                        root(qstat[(p - 3) % 2])
                    exps(n, 1)
                    if p == 1 and b + 1 < B:
                        root(kstat)
                    if n:
                        near_reciprocal(n - 1)
                    if n + 1 < B * PAIRS and p == PAIRS - 1:
                        keep_qst(n + 1)
                    if p == PAIRS - 1 and b + 2 < B:
                        root(stat)
                    end(b + 1, p)
                    if p == 3 and b:
                        root(stat)
                    if n == 0:
                        root(qstat[0][:, :, 8:16])
                        root(qstat[1][:, :, 8:16])
                    ffn_end(b - 1, p)
            near_reciprocal(B * PAIRS - 1)
            keep_yT(B - 1)
            f = B - 1
            root(stat)
            keep_fxT(f)
            relu_first(f, 0)
            gate_exp(f)
            relu_first(f, 1)
            relu_first(f, 2)
            weight_exp(f)
            relu_second(f, 0)
            relu_first(f, 3)
            relu_second(f, 1)
            relu_first(f, 4)
            relu_second(f, 2)

        @block.vector
        def _(dve):
            links, roots = [0], [0]

            def link(ins):
                links[0] += 1
                ins.then_inc(s_dve, 1)
                dve.wait_ge(s_dve, links[0])

            def ask_root(ins):
                roots[0] += 1
                ins.then_inc(s_sum, 1)
                return roots[0]

            def spread(x, n):
                return x.unsqueeze(2).broadcast_to([P, x.shape[-1], n])

            def centre(src):
                link(dve.reduce_sum(stat[:, 5, :], src, AX.X))
                link(dve.tensor_scalar(stat[:, 6, :], stat[:, 5, :], 1.0 / D, None, ALU.mult))
                link(dve.tensor_tensor(xc[:, :, :], src, spread(stat[:, 6, :], D), ALU.subtract))

            def deviation():
                link(dve.tensor_tensor(sq[:, :, :], xc[:, :, :], xc[:, :, :], ALU.mult))
                link(dve.reduce_sum(stat[:, 0, :], sq[:, :, :], AX.X))
                return ask_root(dve.tensor_scalar(stat[:, 1, :], stat[:, 0, :], D * LN_EPS, None, ALU.add))

            def refine(asked, st):
                dve.wait_ge(s_root, asked)
                link(dve.tensor_tensor(st[:, 0, :], st[:, 2, :], st[:, 2, :], ALU.mult))
                link(dve.tensor_tensor(st[:, 0, :], st[:, 0, :], st[:, 1, :], ALU.mult))
                link(dve.scalar_tensor_tensor(st[:, 4, :], st[:, 0, :], 3.0, st[:, 2, :], ALU.subtract, ALU.mult))

            def norm_scale(asked, n):
                refine(asked, stat)
                if n:
                    dve.wait_ge(s_xTp, n)
                dve.scalar_tensor_tensor(xn[:, :, :], xc[:, :, :], -0.5 * float(D) ** 0.5, spread(stat[:, 4, :], D),
                                         ALU.mult, ALU.mult).then_inc(s_xn, 1)

            def embed(b):
                if b:
                    dve.wait_ge(s_h0, b * (C - 1))
                    centre(h[:, b, :, :])
                    return deviation()
                dve.wait_ge(s_emb[b], 16 * SLOTS)
                dve.wait_ge(s_halo[b], 16)
                dve.wait_ge(s_halo0[b], 16)
                rows = emb[:, b, :, :].rearrange("p k c -> p (k c)")
                shifted = bass.AP(tensor=rows.tensor, offset=rows.offset,
                                  ap=[rows.ap[0], [C * D, SLOTS], [1, D], [C * D + D, C]])
                link(dve.reduce_sum(h[:, b, :, :], shifted, AX.X))
                centre(h[:, b, :, :])
                return deviation()

            def key_sums(b):
                dve.wait_ge(s_kv, b + 1)
                kv = QP0[:, :].rearrange("p (t c) -> p t c", c=2 * D)
                if b:
                    dve.wait_ge(s_ktok, 2 * b)
                if b >= 2:
                    dve.wait_ge(s_pv, (b - 1) * PAIRS)
                dve.tensor_copy(v[b % 2][:, :, :], kv[:, :, D:2 * D]).then_inc(s_kv_read, 1)
                ins = dve.tensor_copy(kq[:, 0], kv[:, :, 0:D])
                ins.then_inc(s_kv_read, 1)
                dve.wait_ge(s_kv_read, 2 * b + 2)
                link(dve.tensor_tensor(kq[:, 1], kq[:, 0], kq[:, 0], ALU.mult))
                link(dve.reduce_sum(kstat[:, 0, :], kq[:, 1], AX.X))
                return ask_root(dve.tensor_scalar(kstat[:, 1, :], kstat[:, 0, :], D * RMS_EPS, None, ALU.add))

            def key_norm(asked, b):
                refine(asked, kstat)
                dve.scalar_tensor_tensor(kq[:, 1], kq[:, 0], -0.5, spread(kstat[:, 4, :], D),
                                         ALU.mult, ALU.mult).then_inc(s_kn, 1)

            def query_sums(b, t, halves=(0, 1)):
                n = unit(b, t, halves[-1])
                heads = slice(8 * halves[0], 8 * halves[-1] + 8)
                q = qstat[t % 2][:, :, heads]
                dve.wait_ge(s_qsq, n + 1)
                ins = dve.reduce_sum(q[:, 0, :], qsq[t % 2][:, heads, :], AX.X)
                ins.then_inc(s_qsum, len(halves))
                dve.wait_ge(s_qsum, n + 1)
                return ask_root(dve.tensor_scalar(q[:, 1, :], q[:, 0, :], D * RMS_EPS, None, ALU.add))

            def query_scale(asked, b, t, halves=(0, 1)):
                refine(asked, qstat[t % 2][:, :, 8 * halves[0]:8 * halves[-1] + 8])
                if b:
                    dve.wait_ge(s_qr, PAIRS * b)
                for i in halves:
                    dve.scalar_tensor_tensor(qn[:, t, 8 * i:8 * i + 8, :],
                                             q_bank(b, t, i)[:, :].rearrange("p (h d) -> p h d", d=D), -0.5,
                                             spread(qstat[t % 2][:, 4, 8 * i:8 * i + 8], D),
                                             ALU.mult, ALU.mult).then_inc(s_qs, 1)

            def note(ins):
                links[0] += 1
                return ins.then_inc(s_dve, 1)

            def turn(b, first, pairs=2):
                n, heads = PAIRS * b + first, slice(2 * first, 2 * (first + pairs))
                src, shape = qn[:, :, heads, :], [P, TILES, 2 * pairs, D]
                cos, sin = [ec(x).rearrange("p (t d) -> p t d", d=D).unsqueeze(2) for x in ("cos", "sin")]
                by_cos, by_sin = [x[:, 0:TILES * 2 * pairs * D].rearrange("p (t h d) -> p t h d", t=TILES, d=D)
                                  for x in (qcos, qsin)]
                dve.wait_ge(s_qs, unit(b, TILES - 1, 2 * first // 8) + 1)
                if n:
                    dve.wait_ge(s_qr, n)
                for e in range(2):
                    note(dve.tensor_tensor(by_sin[:, :, :, e::2], src[:, :, :, 1 - e::2],
                                           sin[:, :, :, e::2].broadcast_to(shape[:3] + [D // 2]), ALU.mult))
                link(dve.tensor_tensor(by_cos, src, cos.broadcast_to(shape), ALU.mult))
                if b:
                    dve.wait_ge(s_qt, n - PAIRS + pairs)
                dve.tensor_tensor(qs[:, :, heads, :], by_cos, by_sin, ALU.add).then_inc(s_qr, pairs)

            asked = {}

            def middle(b, slot):
                if slot == 7 and b + 1 < B:
                    asked["x"] = embed(b + 1)
                if b < B:
                    if slot == 0:
                        norm_scale(asked["x"], NORM["x", b])
                    elif slot == 1:
                        asked["k"] = key_sums(b)
                    elif slot == 2:
                        key_norm(asked["k"], b)
                    elif 3 <= slot <= 6:
                        t = slot - 3
                        query_scale(query_sums(b, t), b, t)
                        ffn_middle(b - 1, slot)

            before = lc("before").rearrange("p (e f) -> p e f", f=E)

            def gate_max(f):
                dve.wait_ge(s_g, f + 1)
                logits = ffn_bank(f, "G")[:, 0:SLOTS * E].rearrange("p (j e) -> p j e", e=E)
                ins = dve.tensor_copy(ge[:, 7], logits)
                ins.then_inc(s_gc, 1)
                dve.wait_ge(s_gc, f + 1)
                link(dve.reduce_max(gst[:, 0, :], ge[:, 7], AX.X))
                dve.tensor_tensor(ge[:, 0], ge[:, 7], spread(gst[:, 0, :], E), ALU.subtract).then_inc(s_gx, 1)

            def gate_probabilities(f):
                dve.wait_ge(s_ge, f + 1)
                link(dve.reduce_sum(gst[:, 1, :], ge[:, 1], AX.X))
                link(dve.reciprocal(gst[:, 4, :], gst[:, 1, :]))
                link(dve.tensor_tensor(ge[:, 2], ge[:, 1], spread(gst[:, 4, :], E), ALU.mult))
                link(dve.reduce_max(gst[:, 2, :], ge[:, 2], AX.X))
                dve.tensor_tensor(ge[:, 3], ge[:, 2], spread(gst[:, 2, :], E), ALU.subtract).then_inc(s_gp, 1)
                dve.wait_ge(s_gp, f + 1)

            def gate_ranks(f):
                if f == 0:
                    dve.wait_ge(s_late, 16)
                mine = ge[:, 2].unsqueeze(3).broadcast_to([P, SLOTS, E, E])
                other = ge[:, 2].unsqueeze(2).broadcast_to([P, SLOTS, E, E])
                link(dve.tensor_tensor(gcmp[:, 0], other, mine, ALU.is_gt))
                link(dve.tensor_tensor(gcmp[:, 1], other, mine, ALU.is_equal))
                link(dve.tensor_tensor(gcmp[:, 2], gcmp[:, 1], before.unsqueeze(1).broadcast_to([P, SLOTS, E, E]),
                                       ALU.mult))
                link(dve.tensor_tensor(gcmp[:, 1], gcmp[:, 0], gcmp[:, 2], ALU.add))
                link(dve.reduce_sum(ge[:, 5], gcmp[:, 1], AX.X))
                link(dve.tensor_scalar(ge[:, 6], ge[:, 5], 1.5, None, ALU.is_lt))

            def gate_weights(f):
                dve.wait_ge(s_gw, f + 1)
                link(dve.tensor_tensor(ge[:, 5], ge[:, 4], ge[:, 6], ALU.mult))
                link(dve.reduce_sum(gst[:, 3, :], ge[:, 5], AX.X))
                link(dve.reciprocal(gst[:, 5, :], gst[:, 3, :]))
                if f >= 2:
                    dve.wait_ge(s_base, 6 * (f - 1))
                dve.tensor_tensor(gw[f % 2][:, :, :], ge[:, 5], spread(gst[:, 5, :], E), ALU.mult).then_inc(s_gwt, 1)
                dve.wait_ge(s_gwt, f + 1)

            def weigh_experts(f):
                for i in range(2):
                    dve.wait_ge(s_f3, 3 * f + i + 1)
                    ins = dve.tensor_tensor(
                        eo2[:, :, 2 * i:2 * i + 2, :],
                        ffn_bank(f, f"L{i + 1}")[:, :].rearrange("p (j e d) -> p j e d", e=2, d=D),
                        gw[f % 2][:, :, 2 * i:2 * i + 2].unsqueeze(3).broadcast_to([P, SLOTS, 2, D]), ALU.mult)
                    ins.then_inc(s_l3, 1)
                dve.wait_ge(s_l3, 3 * f + 2)

            def finish(f):
                link(dve.reduce_sum(fsum[:, 0], eo2[:, :, :, :].rearrange("p j e d -> p j d e"), AX.X))
                dve.wait_ge(s_f3, 3 * f + 3)
                dve.wait_ge(s_base, 6 * f + 6)
                dve.tensor_tensor(fsum[:, 1], ffn_bank(f, "L0")[:, 0:SLOTS * D].rearrange("p (j d) -> p j d", d=D),
                                  base[:, 4], ALU.add).then_inc(s_l3, 1)
                dve.wait_ge(s_l3, 3 * f + 3)
                dve.tensor_tensor(h[:, f, :, :], fsum[:, 0], fsum[:, 1], ALU.add).then_inc(s_fin, 1)

            def ffn_middle(b, slot):
                f = b - 1 if slot >= 2 else b - 2
                if f >= 0:
                    if slot == 0:
                        weigh_experts(f)
                    elif slot == 3:
                        centre(h[:, f, :, :])
                        asked["f"] = deviation()
                    elif slot == 4:
                        norm_scale(asked["f"], NORM["f", f])
                    elif slot == 5:
                        gate_max(f)
                    elif slot == 6:
                        gate_probabilities(f)
                    elif slot == 7:
                        gate_weights(f)

            def ffn_end(b, slot):
                f = b - 1 if slot >= 2 else b - 2
                if f >= 0:
                    if slot == 1:
                        finish(f)
                    elif slot == 6:
                        gate_ranks(f)

            def divide(n):
                dve.wait_ge(s_r0, n + 1)
                link(dve.tensor_tensor(nw[:, :], DN[:, :], r0[:, :], ALU.mult))
                link(dve.scalar_tensor_tensor(nw[:, :], nw[:, :], 2.0, r0[:, :], ALU.subtract, ALU.mult))
                b = n // PAIRS
                if b:
                    dve.wait_ge(s_yTp, b)
                dve.scalar_tensor_tensor(oT[:, n % PAIRS, :], OP[:, :], -1.0, nw[:, :],
                                         ALU.mult, ALU.mult).then_inc(s_oT, 1)

            def add_y(b):
                dve.wait_ge(s_y, b + 1)
                dve.tensor_tensor(h[:, b, :, :], h[:, b, :, :],
                                  y_banks(b)[1][:, 0:SLOTS * D].rearrange("p (j d) -> p j d", d=D), ALU.add).then_inc(s_h, 1)

            dve.memset(qst[1][:, :], 1.0).then_inc(s_warm, 1)
            for i in range(2):
                for a in range(2):
                    dve.memset(kst[i][D * (1 - a):D * (1 - a) + D, a, :], 0.0).then_inc(s_warm, 1)
            norm_scale(embed(0), 0)
            dve.wait_ge(s_early, 16)
            link(dve.tensor_tensor(gs[:, :], ec("qn"), ec("kn"), ALU.mult))
            link(dve.tensor_scalar(gs[:, :], gs[:, :], float(D) ** 0.5, None, ALU.mult))
            link(dve.tensor_scalar(sq[:, 1, :], gs[:, :], -1.0, None, ALU.mult))
            link(dve.tensor_tensor(sq[:, 0, :], gs[:, :], sq[:, 1, :], ALU.max))
            link(dve.reduce_max(shift[:, 0:1], sq[:, 0, :], AX.X))
            link(dve.tensor_scalar(shift[:, 1:2], shift[:, 0:1], -1.0, 80.0, ALU.mult, ALU.add))
            dve.tensor_scalar(shift[:, 1:2], shift[:, 1:2], 0.0, None, ALU.min).then_inc(s_shift, 1)
            key_root = key_sums(0)
            sums = {0: query_sums(0, 0, (0,))}
            key_norm(key_root, 0)
            for t in range(TILES):
                if t + 1 < TILES:
                    sums[t + 1] = query_sums(0, t + 1, (0,))
                query_scale(sums[t], 0, t, (0,))
            turn(0, 0, 1)
            asked["x"] = embed(1)
            sums = [query_sums(0, t, (1,)) for t in range(2)]
            for b in range(B):
                for p in range(PAIRS):
                    n = b * PAIRS + p
                    if p == 2 and b:
                        add_y(b - 1)
                    if p == 7 and b + 1 < B:
                        turn(b + 1, 0)
                    if p == 7 or b == B - 1 and p >= 3:
                        ffn_middle(b, p)
                    middle(b + 1, p)
                    if n == 0:
                        turn(0, 1, 1)
                    if n < 2:
                        for t in (2 * n, 2 * n + 1):
                            query_scale(sums[t], 0, t, (1,))
                    if p < 3:
                        turn(b, 2 * p + 2)
                    if p == 0:
                        ffn_middle(b, p)
                    if n == 0:
                        sums += [query_sums(0, t, (1,)) for t in range(2, TILES)]
                    if n:
                        divide(n - 1)
                    ffn_end(b, p)
            f = B - 1
            weigh_experts(f - 1)
            divide(B * PAIRS - 1)
            finish(f - 1)
            add_y(f)
            dve.wait_ge(s_h, B)
            centre(h[:, f, :, :])
            norm_scale(deviation(), NORM["f", f])
            gate_max(f)
            gate_probabilities(f)
            gate_ranks(f)
            gate_weights(f)
            weigh_experts(f)
            finish(f)

        @block.tensor
        def _(pe):
            def transpose_x(kind, b):
                n = NORM[kind, b]
                pe.wait_ge(s_xn, n + 1)
                if n == 0:
                    pe.wait_ge(s_early, 16)
                elif kind == "x":
                    if b == 1:
                        pe.wait_ge(s_qs, TILES + 1)
                    pe.wait_ge(s_kst, 2 * b)
                    if b > 2:
                        pe.wait_ge(s_f2r, 3 * (b - 3) + 1)
                elif b:
                    pe.wait_ge(s_l3, 3 * b if b < B - 1 else 3 * b - 2)
                dst = QP0 if kind == "x" else ffn_bank(b, "T")
                for j in range(SLOTS):
                    last = pe.transpose(dst[0:D, j * P:(j + 1) * P], xn[:, j, :], ident)
                last.then_inc(s_xTp, 1)

            def project_kv(b):
                pe.wait_ge(s_xT, b + 1)
                pe.wait_ge(s_w64, 32)
                for t in range(TILES):
                    last = pe.matmul(QP0[:, t * 2 * D:(t + 1) * 2 * D], xT[0:D, t * P:(t + 1) * P], wc("wkv"),
                                     start=True, stop=True)
                last.then_inc(s_kv, 1)

            def project_q(b, t, halves=(0, 1)):
                if b and t == 0:
                    pe.wait_ge(s_kv_read, 2 * b + 2)
                    if b >= 2:
                        pe.wait_ge(s_h, b - 1)
                for i in halves:
                    if b:
                        pe.wait_ge(s_qs, unit(b, t, 0))
                    elif i == 1 and t == 0:
                        pe.wait_ge(s_kv_read, 2)
                    elif i == 1 and t == 3:
                        pe.wait_ge(s_qs, 3)
                    pe.matmul(q_bank(b, t, i)[:, :], xT[0:D, t * P:(t + 1) * P], wc("wq")[:, 512 * i:512 * i + 512],
                              start=True, stop=True).then_inc(s_q, 1)

            def transpose_k(b):
                pe.wait_ge(s_ktok, 2 * b + 2)
                if b:
                    pe.wait_ge(s_qs, 2 * TILES * (b + 1))
                else:
                    pe.wait_ge(s_qs, 1)
                for t in range(TILES):
                    last = pe.transpose(k_bank(b)[:, t * P:(t + 1) * P], ktok[:, t].rearrange("p a d -> p (a d)"), ident)
                last.then_inc(s_kp, 1)

            def end(b, slot):
                if b < B:
                    if slot == 0:
                        transpose_x("x", b)
                    elif 2 <= slot <= 5:
                        project_q(b, slot - 2)
                    elif slot == 6:
                        transpose_k(b)

            def transpose_q(n):
                b, p = n // PAIRS, n % PAIRS
                if p % 2 == 0 or n == 1:
                    pe.wait_ge(s_qr, n + 1 if n < 2 else n + 2)
                if n:
                    pe.wait_ge(s_qst, n)
                for t in range(TILES):
                    src = qs[:, t, 2 * p:2 * p + 2, :].rearrange("p a d -> p (a d)")
                    last = pe.transpose(QT[:, t * P:(t + 1) * P], src, ident)
                last.then_inc(s_qt, 1)

            def scores(n):
                if n % H == 0:
                    pe.wait_ge(s_kst, 2 * (n // H + 1))
                pe.wait_ge(s_qst, n // 2 + 1)
                for half in range(2):
                    u = 2 * n + half
                    if u >= 2:
                        pe.wait_ge(s_p, u - 1)
                    bk = SC[u % 2]
                    for kt, c, w in HALVES[half]:
                        for odd in range(2):
                            o = D * odd
                            seen = slice(o, min(o + P + D, w))
                            last = pe.matmul(bk[o:o + D, c + seen.start:c + seen.stop],
                                             kst[n // H % 2][:, n % 2, kt * P + o:kt * P + o + D],
                                             qst[n // 2 % 2][:, kt * P + seen.start:kt * P + seen.stop],
                                             start=True, stop=True, skip_group_check=True)
                    last.then_inc(s_sc, 1)

            def weigh(n):
                if n % PAIRS == 0:
                    pe.wait_ge(s_kv_read, 2 * (n // PAIRS) + 1)
                pe.wait_ge(s_m, 4 * n + 4)
                if n:
                    pe.wait_ge(s_oT, n)
                else:
                    pe.wait_ge(s_qs, TILES)
                for t in range(TILES):
                    w = WIN if t < TILES - 1 else P
                    for hh in range(2):
                        pe.matmul(OP[D * hh:D * hh + D, t * P:t * P + w], v[n // PAIRS % 2][:, t, :],
                                  pT[n % 2][:, hh, t * WIN:t * WIN + w],
                                  start=(t == 0), stop=(t == TILES - 1), skip_group_check=True)
                if n == 0:
                    pe.wait_ge(s_qs, 2 * TILES - 1)
                for hh in range(2):
                    pe.matmul(DN[D * hh:D * hh + D, 0:P], ones[:, :], pT[n % 2][:, hh, 0:P], start=True, stop=False,
                              skip_group_check=True)
                pe.wait_ge(s_ps, 2 * n + 2)
                for hh in range(2):
                    last = pe.matmul(DN[D * hh:D * hh + D, P:S], ones[:, :],
                                     pS[n % 2][:, hh].rearrange("p t w -> p (t w)"), start=False, stop=True,
                                     skip_group_check=True)
                last.then_inc(s_pv, 1)

            def output_T(b, quads=range(PAIRS // 2)):
                if b == 0:
                    pe.wait_ge(s_late, 16)
                if b < B - 1:
                    pe.wait_ge(s_oT, (b + 1) * PAIRS)
                    if b:
                        pe.wait_ge(s_l3, 3 * b - 1)
                else:
                    pe.wait_ge(s_qst, B * PAIRS)
                bk = y_banks(b)[0]
                for q in quads:
                    if b == B - 1:
                        pe.wait_ge(s_oT, b * PAIRS + 2 * q + 2)
                    for odd in range(2):
                        p = 2 * q + odd
                        last = pe.matmul(bk[D * odd:D * odd + D, :], lc("wo")[:, p * D:(p + 1) * D], oT[:, p, :],
                                         start=(q == 0), stop=(q == PAIRS // 2 - 1), skip_group_check=True)
                if q == PAIRS // 2 - 1:
                    last.then_inc(s_yTp, 1)

            def output(b):
                pe.wait_ge(s_yT, b + 1)
                if b == B - 1:
                    pe.wait_ge(s_f2r, 3 * b - 2)
                yv = yT[:, :].rearrange("d (p j) -> d j p", j=SLOTS)
                for j in range(SLOTS):
                    last = pe.matmul(y_banks(b)[1][:, j * D:(j + 1) * D], yv[:, j, :], ec("ident2"),
                                     start=True, stop=True)
                last.then_inc(s_y, 1)

            def keep_warm(bk, data, count):
                for _ in range(count):
                    pe.matmul(bk[0:D, :], ones[:, :], data, start=True, stop=True)

            def gates(f):
                pe.wait_ge(s_fxT, f + 1)
                bk = ffn_bank(f, "G")
                for j in range(SLOTS):
                    last = pe.matmul(bk[:, j * E:(j + 1) * E], fxT[:, j * P:(j + 1) * P], wc("gW", D + 1),
                                     start=True, stop=True)
                last.then_inc(s_g, 1)

            def first(f, i):
                bk = ffn_bank(f, f"F{i}")
                if f < B - 1 and i == 0:
                    pe.wait_ge(s_gc, f + 1)
                elif f < B - 1 and i == 3:
                    pe.wait_ge(s_qs, min(f + 3, B) * 2 * TILES)
                    pe.wait_ge(s_h, f + 1)
                elif f < B - 1:
                    pe.wait_ge(s_f1r, (E + 1) * f + min(i, 3))
                elif i == 2:
                    pe.wait_ge(s_l3, 3 * f)
                if i == 0:
                    last = pe.matmul(bk[0:SH1, :], wc("sW1"), fxT[0:D, :], start=True, stop=True)
                else:
                    last = pe.matmul(bk[:, :], wc("eW1")[:, (i - 1) * EH1:i * EH1], fxT[0:D, :], start=True, stop=True)
                last.then_inc(s_f1, 1)

            def second(f, i):
                bk = ffn_bank(f, f"S{i}")
                pe.wait_ge(s_f1r, (E + 1) * f + (1, 3, 5)[i])
                if f < B - 1 and i == 0:
                    pe.wait_ge(s_kst, 2 * min(f + 3, B))
                elif f < B - 1 and i == 1:
                    pe.wait_ge(s_f1r, (E + 1) * (f + 1))
                if f == B - 1 and i == 1:
                    pe.wait_ge(s_gc, B)
                if i == 0:
                    last = pe.matmul(bk[:, :], wc("sW2", SH1), hs1[:, :], start=True, stop=True)
                for k in range(2 if i else 0):
                    e = 2 * (i - 1) + k
                    last = pe.matmul(bk[D * k:D * k + D, :], lc("eW2")[:, e * EH2:(e + 1) * EH2],
                                     he1[:, e, :], start=True, stop=True)
                last.then_inc(s_f2, 1)

            def third(f, i):
                bk = ffn_bank(f, f"L{i}")
                pe.wait_ge(s_f2r, 3 * f + i + 1)
                if i == 0:
                    pe.wait_ge(s_l3, 3 * f + 1)
                for j in range(SLOTS):
                    if i == 0:
                        last = pe.matmul(bk[:, j * D:(j + 1) * D], hs2[:, j * P:(j + 1) * P], lc("sW3"),
                                         start=True, stop=True)
                    else:
                        last = pe.matmul(bk[:, j * P:(j + 1) * P], he2[:, i - 1, j * P:(j + 1) * P],
                                         lc("eW3")[:, (i - 1) * P:i * P], start=True, stop=True)
                last.then_inc(s_f3, 1)

            def ffn_middle(b, slot):
                f = b - 1 if slot >= 2 else b - 2
                if f >= 0:
                    if slot == 0:
                        third(f, 1)
                        third(f, 2)
                    elif slot == 5:
                        gates(f)
                    elif slot == 6:
                        first(f, 1)
                    elif slot == 7:
                        first(f, 4)
                        second(f, 0)

            def ffn_end(b, slot):
                f = b - 1 if slot >= 2 else b - 2
                if f >= 0:
                    if slot == 0:
                        third(f, 0)
                    elif slot == 4:
                        transpose_x("f", f)
                    elif slot == 5:
                        first(f, 0)
                    elif slot == 6:
                        first(f, 2)
                        first(f, 3)
                    elif slot == 7:
                        second(f, 1)
                        second(f, 2)

            pe.wait_ge(s_ones, 2)
            pe.wait_ge(s_warm, 1)
            keep_warm(DN, qst[1][:, :], 16)
            transpose_x("x", 0)
            project_kv(0)
            for t in range(TILES):
                project_q(0, t, (0,))
            tables = early[:, EARLY["cos"][0]:EARLY["cos"][0] + S]
            for t in range(TILES):
                if t == TILES - 1:
                    keep_warm(QT, tables, 6)
                project_q(0, t, (1,))
            transpose_k(0)
            transpose_q(0)
            keep_warm(OP, tables, 1)
            pe.wait_ge(s_warm, 5)
            for b in range(B):
                for p in range(PAIRS):
                    n = b * PAIRS + p
                    scores(2 * n)
                    if n == 0:
                        keep_warm(OP, tables, 2)
                    if n + 1 < B * PAIRS and p < PAIRS - 1:
                        transpose_q(n + 1)
                    if p == 1 and b + 1 < B:
                        project_kv(b + 1)
                    if p == 1 and b:
                        output_T(b - 1)
                    ffn_middle(b, p)
                    scores(2 * n + 1)
                    if n:
                        weigh(n - 1)
                    if n + 1 < B * PAIRS and p == PAIRS - 1:
                        transpose_q(n + 1)
                    end(b + 1, p)
                    if p == 1 and b:
                        output(b - 1)
                    ffn_end(b, p)
            f = B - 1
            third(f - 1, 1)
            third(f - 1, 2)
            output_T(f, range(PAIRS // 2 - 1))
            weigh(B * PAIRS - 1)
            third(f - 1, 0)
            spare = SC[0]
            keep_warm(spare, tables, 3)
            output_T(f, range(PAIRS // 2 - 1, PAIRS // 2))
            keep_warm(spare, tables, 1)
            output(f)
            keep_warm(spare, tables, 5)
            transpose_x("f", f)
            keep_warm(spare, tables, 1)
            gates(f)
            first(f, 0)
            first(f, 1)
            first(f, 2)
            second(f, 0)
            first(f, 3)
            second(f, 1)
            first(f, 4)
            third(f, 1)
            second(f, 2)
            third(f, 2)
            third(f, 0)


def _tables():
    f32 = np.float32
    freqs = np.power(f32(10000.0), (f32(-2.0) * np.arange(D // 2, dtype=f32) / f32(D)).astype(f32)).astype(f32)
    theta = (np.arange(S, dtype=f32)[:, None] * freqs[None, :]).astype(f32)
    cos, sin = np.repeat(np.cos(theta), 2, 1), np.repeat(np.sin(theta), 2, 1)
    sign = np.tile(np.array([-1.0, 1.0], f32), D // 2)
    by_tile = lambda a: a.reshape(TILES, P, D).transpose(1, 0, 2).reshape(P, TILES * D)
    e = np.arange(E)
    return {
        "ident": np.eye(P, dtype=f32), "cos": by_tile(cos), "sin": by_tile(sin * sign), "ident2": np.tile(np.eye(D, dtype=f32), (2, 1)),
        "before": np.tile((e[None, :] < e[:, None]).astype(f32).reshape(1, E * E), (P, 1)),
    }


def _pack(where, width, rows, parts):
    a = np.zeros((rows, width), np.float32)
    for name, part in parts.items():
        o, w = where[name]
        assert part.shape[1] == w, name
        a[:part.shape[0], o:o + w] = part
    return a


def kernel(**inputs):
    import concourse.bacc as bacc
    from concourse.bass_utils import run_bass_kernel_spmd

    i = {k.replace("L0_", ""): np.asarray(a) for k, a in inputs.items()}
    t = _tables()
    rows = lambda a: np.tile(a.reshape(1, -1), (P, 1))
    early = _pack(EARLY, EARLY_W, P, {**{k: t[k] for k in ("ident", "cos", "sin", "ident2")},
                                      "qn": rows(i["attn_q_norm_w"]), "kn": rows(i["attn_k_norm_w"])})
    eW3 = np.zeros((P, 2, 2, D), np.float32)
    for e in range(E):
        eW3[D * (e % 2):D * (e % 2) + D, e // 2, e % 2] = i["ffn_eW3"][e]
    late = _pack(LATE, LATE_W, P, {
        "wo": i["attn_wo"].T.reshape(PAIRS, P, D).transpose(1, 0, 2).reshape(P, -1),
        "eW2": i["ffn_eW2"].transpose(1, 0, 2).reshape(EH1, -1), "sW3": i["ffn_sW3"], "eW3": eW3.reshape(P, -1),
        "eb1": i["ffn_eb1"].T, "eb2": i["ffn_eb2"].reshape(2, P).T, "sb2": i["ffn_sb2"].reshape(-1, 1),
        "sb1": i["ffn_sb1"].reshape(-1, 1), "eb3": rows(i["ffn_eb3"]), "sb3": rows(i["ffn_sb3"]),
        "before": t["before"]})
    w64 = _pack(W64, W64_W, D, {
        "wq": i["attn_wq"].T, "wkv": i["attn_wkv"].T, "sW1": i["ffn_sW1"],
        "eW1": i["ffn_eW1"].transpose(1, 0, 2).reshape(D, -1), "sW2": i["ffn_sW2"], "gW": i["ffn_gW"]})
    arrays = {
        "tok": np.ascontiguousarray(i["x"].reshape(B, P, SLOTS).transpose(1, 0, 2).reshape(P, B * SLOTS)),
        "table": np.ascontiguousarray(i["tok_emb_table"].reshape(-1, C * D)),
        "early": early, "late": late, "w64": w64,
        "gb": np.ascontiguousarray(i["ffn_gb"].reshape(1, E)),
    }
    nc = bacc.Bacc("TRN2", target_bir_lowering=False, num_devices=1)
    aps = [nc.dram_tensor("in_" + n, a.shape, mybir.dt.from_np(a.dtype), kind="ExternalInput").ap()
           for n, a in arrays.items()]
    out = nc.dram_tensor("out_h", (B, S, D), FP32, kind="ExternalOutput").ap()
    build(nc, *aps, out)
    r = run_bass_kernel_spmd(nc, [{"in_" + n: a for n, a in arrays.items()}], core_ids=[0])
    return r.results[0]["out_h"]
```
